# Optimizing a Trainium2 kernel written in Bass

```python
import numpy as np
import jax
import jax.numpy as jnp

def _softmax(x, axis=-1):
    return jax.nn.softmax(x, axis=axis)

def _gelu(x):
    return jax.nn.gelu(x, approximate=True)

def _silu(x):
    return jax.nn.silu(x)

def _sigmoid(x):
    return jax.nn.sigmoid(x)

def _layernorm(x, axis=-1, eps=1e-05):
    m = jnp.mean(x, axis=axis, keepdims=True)
    v = jnp.var(x, axis=axis, keepdims=True)
    return (x - m) / jnp.sqrt(v + eps)

def _scatter_add(tgt, idx, src, axis=0):
    return tgt.at[idx].add(src)

def _segment_sum(src, seg, n):
    return jax.ops.segment_sum(src, seg, n)
kernel_name = 'mk_pixart_seq_d2_seqx_r4_2185ea'

def setup_inputs(seed: int=0):
    np.random.seed(seed)
    _w = jnp.asarray

    def _rec_inputs():
        import jax
        import jax.numpy as jnp
        _rk = jax.random.key(seed)
        x = -0.0002928 + 1 * jax.random.normal(jax.random.fold_in(_rk, 1), (8, 256, 256), jnp.float32)
        _lenS = 256 - jax.random.randint(jax.random.fold_in(_rk, 7), (8,), 0, max(1, 256 // 4) + 1, jnp.int32)
        _lenS2 = 77 - jax.random.randint(jax.random.fold_in(_rk, 8), (8,), 0, max(1, 77 // 4) + 1, jnp.int32)
        cond_1024 = 0.0061147 + 1.02565 * jax.random.normal(jax.random.fold_in(_rk, 11), (8, 256), jnp.float32)
        _ctx_1024P = jax.random.normal(jax.random.fold_in(_rk, 12), (8, 16, 256), jnp.float32)
        _ctx_1024c = jax.random.dirichlet(jax.random.fold_in(_rk, 512), 0.3 * jnp.ones((16,), jnp.float32), (8, 77))
        _ctx_1024t = jnp.einsum('bsk,bkd->bsd', _ctx_1024c, _ctx_1024P)
        _ctx_1024t = _ctx_1024t * jax.lax.rsqrt(jnp.mean(jnp.square(_ctx_1024t)) + 1e-12) * 0.953939
        ctx_1024 = -0.00265004 + 0.998804 * (_ctx_1024t + 0.3 * jax.random.normal(jax.random.fold_in(_rk, 612), (8, 77, 256), jnp.float32))
        return (x, cond_1024, ctx_1024)
    x, cond_1024, ctx_1024 = _rec_inputs()

    def _L0_xcond_setup():
        import jax, jax.numpy as jnp
        import numpy as np
        LN_EPS = 1e-06

        def _ln(x):
            mu = jnp.mean(x, axis=-1, keepdims=True)
            var = jnp.var(x, axis=-1, keepdims=True)
            return (x - mu) * jax.lax.rsqrt(var + LN_EPS)
        key = jax.random.key(seed)
        H, NH = (256, 16)
        B, N, S = (4, 256, 77)
        MLP = int(H * 4.0)
        ks = jax.random.split(key, 20)
        s = 1.0 / np.sqrt(H)
        return {'x': jax.random.normal(ks[0], (B, N, H), jnp.float32), 'c': jax.random.normal(ks[1], (B, H), jnp.float32), 'context': jax.random.normal(ks[2], (B, S, H), jnp.float32), 'W_mod': jax.random.normal(ks[3], (H, 6 * H), jnp.float32) * s, 'b_mod': jnp.zeros((6 * H,), jnp.float32), 'W_qkv': jax.random.normal(ks[4], (H, 3 * H), jnp.float32) * s, 'b_qkv': jnp.zeros((3 * H,), jnp.float32), 'W_proj': jax.random.normal(ks[5], (H, H), jnp.float32) * s, 'b_proj': jnp.zeros((H,), jnp.float32), 'W_qc': jax.random.normal(ks[6], (H, H), jnp.float32) * s, 'b_qc': jnp.zeros((H,), jnp.float32), 'W_kvc': jax.random.normal(ks[7], (H, 2 * H), jnp.float32) * s, 'b_kvc': jnp.zeros((2 * H,), jnp.float32), 'W_cproj': jax.random.normal(ks[8], (H, H), jnp.float32) * s, 'b_cproj': jnp.zeros((H,), jnp.float32), 'W_mlp1': jax.random.normal(ks[9], (H, MLP), jnp.float32) * s, 'b_mlp1': jnp.zeros((MLP,), jnp.float32), 'W_mlp2': jax.random.normal(ks[10], (MLP, H), jnp.float32) * (1.0 / np.sqrt(MLP)), 'b_mlp2': jnp.zeros((H,), jnp.float32)}
    _L0_xcond_all = _L0_xcond_setup()
    _L0_xcond_in = {k: v for k, v in _L0_xcond_all.items() if k in ('W_mod', 'b_mod', 'W_qkv', 'b_qkv', 'W_proj', 'b_proj', 'W_qc', 'b_qc', 'W_kvc', 'b_kvc', 'W_cproj', 'b_cproj', 'W_mlp1', 'b_mlp1', 'W_mlp2', 'b_mlp2')}
    del _L0_xcond_all

    def _L1_xcond_setup():
        import jax, jax.numpy as jnp
        import numpy as np
        import math
        D_MODEL = 256
        N_HEADS = 16
        HEAD_DIM = D_MODEL // N_HEADS
        D_FF = 1024
        EPS = 1e-05
        ROPE_BASE = 10000.0

        def _rope(t):
            L, Dh = (t.shape[1], t.shape[-1])
            half = Dh // 2
            inv_freq = 1.0 / ROPE_BASE ** (jnp.arange(half, dtype=t.dtype) / half)
            ang = jnp.arange(L, dtype=t.dtype)[:, None] * inv_freq[None, :]
            cos = jnp.cos(ang)[None, :, None, :]
            sin = jnp.sin(ang)[None, :, None, :]
            t1, t2 = (t[..., :half], t[..., half:])
            return jnp.concatenate([t1 * cos - t2 * sin, t2 * cos + t1 * sin], axis=-1)

        def _adaln(x, emb, w, b):
            e = emb[:, 0, :]
            gb = e @ w.T + b
            gamma, beta = jnp.split(gb, 2, axis=-1)
            mu = x.mean(-1, keepdims=True)
            var = x.var(-1, keepdims=True)
            xn = (x - mu) * jax.lax.rsqrt(var + EPS)
            return xn * (1.0 + gamma[:, None, :]) + beta[:, None, :]

        def _attn(q, k, v):
            scale = 1.0 / math.sqrt(HEAD_DIM)
            scores = jnp.einsum('bqhd,bkhd->bhqk', q, k) * scale
            w = jax.nn.softmax(scores, axis=-1)
            out = jnp.einsum('bhqk,bkhd->bqhd', w, v)
            B, Lq = (out.shape[0], out.shape[1])
            return out.reshape(B, Lq, D_MODEL)
        key = jax.random.key(seed)
        ks = jax.random.split(key, 24)
        s = 0.02
        inp = {'x': jax.random.normal(ks[0], (2, 512, D_MODEL), jnp.float32), 'noise_emb': jax.random.normal(ks[1], (2, 1, D_MODEL), jnp.float32), 'context': jax.random.normal(ks[2], (2, 256, D_MODEL), jnp.float32), 'ln1_w': jax.random.normal(ks[3], (2 * D_MODEL, D_MODEL), jnp.float32) * s, 'ln1_b': jax.random.normal(ks[4], (2 * D_MODEL,), jnp.float32) * s, 'ln2_w': jax.random.normal(ks[5], (2 * D_MODEL, D_MODEL), jnp.float32) * s, 'ln2_b': jax.random.normal(ks[6], (2 * D_MODEL,), jnp.float32) * s, 'ln3_w': jax.random.normal(ks[7], (2 * D_MODEL, D_MODEL), jnp.float32) * s, 'ln3_b': jax.random.normal(ks[8], (2 * D_MODEL,), jnp.float32) * s, 'qkv_w': jax.random.normal(ks[9], (3 * D_MODEL, D_MODEL), jnp.float32) * s, 'sa_out_w': jax.random.normal(ks[10], (D_MODEL, D_MODEL), jnp.float32) * s, 'q_w': jax.random.normal(ks[11], (D_MODEL, D_MODEL), jnp.float32) * s, 'k_w': jax.random.normal(ks[12], (D_MODEL, D_MODEL), jnp.float32) * s, 'v_w': jax.random.normal(ks[13], (D_MODEL, D_MODEL), jnp.float32) * s, 'ca_out_w': jax.random.normal(ks[14], (D_MODEL, D_MODEL), jnp.float32) * s, 'ffn_w1': jax.random.normal(ks[15], (D_FF, D_MODEL), jnp.float32) * s, 'ffn_b1': jax.random.normal(ks[16], (D_FF,), jnp.float32) * s, 'ffn_w2': jax.random.normal(ks[17], (D_MODEL, D_FF), jnp.float32) * s, 'ffn_b2': jax.random.normal(ks[18], (D_MODEL,), jnp.float32) * s}
        return inp
    _L1_xcond_all = _L1_xcond_setup()
    _L1_xcond_in = {k: v for k, v in _L1_xcond_all.items() if k in ('ln1_w', 'ln1_b', 'ln2_w', 'ln2_b', 'ln3_w', 'ln3_b', 'qkv_w', 'sa_out_w', 'q_w', 'k_w', 'v_w', 'ca_out_w', 'ffn_w1', 'ffn_b1', 'ffn_w2', 'ffn_b2')}
    del _L1_xcond_all
    return {'x': x, 'cond_1024': cond_1024, 'ctx_1024': ctx_1024, 'L0_xcond_W_mod': _L0_xcond_in['W_mod'], 'L0_xcond_b_mod': _L0_xcond_in['b_mod'], 'L0_xcond_W_qkv': _L0_xcond_in['W_qkv'], 'L0_xcond_b_qkv': _L0_xcond_in['b_qkv'], 'L0_xcond_W_proj': _L0_xcond_in['W_proj'], 'L0_xcond_b_proj': _L0_xcond_in['b_proj'], 'L0_xcond_W_qc': _L0_xcond_in['W_qc'], 'L0_xcond_b_qc': _L0_xcond_in['b_qc'], 'L0_xcond_W_kvc': _L0_xcond_in['W_kvc'], 'L0_xcond_b_kvc': _L0_xcond_in['b_kvc'], 'L0_xcond_W_cproj': _L0_xcond_in['W_cproj'], 'L0_xcond_b_cproj': _L0_xcond_in['b_cproj'], 'L0_xcond_W_mlp1': _L0_xcond_in['W_mlp1'], 'L0_xcond_b_mlp1': _L0_xcond_in['b_mlp1'], 'L0_xcond_W_mlp2': _L0_xcond_in['W_mlp2'], 'L0_xcond_b_mlp2': _L0_xcond_in['b_mlp2'], 'L1_xcond_ln1_w': _L1_xcond_in['ln1_w'], 'L1_xcond_ln1_b': _L1_xcond_in['ln1_b'], 'L1_xcond_ln2_w': _L1_xcond_in['ln2_w'], 'L1_xcond_ln2_b': _L1_xcond_in['ln2_b'], 'L1_xcond_ln3_w': _L1_xcond_in['ln3_w'], 'L1_xcond_ln3_b': _L1_xcond_in['ln3_b'], 'L1_xcond_qkv_w': _L1_xcond_in['qkv_w'], 'L1_xcond_sa_out_w': _L1_xcond_in['sa_out_w'], 'L1_xcond_q_w': _L1_xcond_in['q_w'], 'L1_xcond_k_w': _L1_xcond_in['k_w'], 'L1_xcond_v_w': _L1_xcond_in['v_w'], 'L1_xcond_ca_out_w': _L1_xcond_in['ca_out_w'], 'L1_xcond_ffn_w1': _L1_xcond_in['ffn_w1'], 'L1_xcond_ffn_b1': _L1_xcond_in['ffn_b1'], 'L1_xcond_ffn_w2': _L1_xcond_in['ffn_w2'], 'L1_xcond_ffn_b2': _L1_xcond_in['ffn_b2']}

def reference(x, cond_1024, ctx_1024, L0_xcond_W_mod, L0_xcond_b_mod, L0_xcond_W_qkv, L0_xcond_b_qkv, L0_xcond_W_proj, L0_xcond_b_proj, L0_xcond_W_qc, L0_xcond_b_qc, L0_xcond_W_kvc, L0_xcond_b_kvc, L0_xcond_W_cproj, L0_xcond_b_cproj, L0_xcond_W_mlp1, L0_xcond_b_mlp1, L0_xcond_W_mlp2, L0_xcond_b_mlp2, L1_xcond_ln1_w, L1_xcond_ln1_b, L1_xcond_ln2_w, L1_xcond_ln2_b, L1_xcond_ln3_w, L1_xcond_ln3_b, L1_xcond_qkv_w, L1_xcond_sa_out_w, L1_xcond_q_w, L1_xcond_k_w, L1_xcond_v_w, L1_xcond_ca_out_w, L1_xcond_ffn_w1, L1_xcond_ffn_b1, L1_xcond_ffn_w2, L1_xcond_ffn_b2):
    import jax
    import jax.numpy as jnp

    def _L0_xcond_ref(x, c, context, W_mod, b_mod, W_qkv, b_qkv, W_proj, b_proj, W_qc, b_qc, W_kvc, b_kvc, W_cproj, b_cproj, W_mlp1, b_mlp1, W_mlp2, b_mlp2):
        import jax, jax.numpy as jnp
        import numpy as np
        LN_EPS = 1e-06

        def _ln(x):
            mu = jnp.mean(x, axis=-1, keepdims=True)
            var = jnp.var(x, axis=-1, keepdims=True)
            return (x - mu) * jax.lax.rsqrt(var + LN_EPS)
        B, N, H = x.shape
        NH = 16
        hd = H // NH
        scale = hd ** (-0.5)
        c_proj = jax.nn.silu(c) @ W_mod + b_mod
        shift_a, scale_a, gate_a, shift_m, scale_m, gate_m = jnp.split(c_proj, 6, axis=-1)

        def modulate(t, shift, sc):
            return t * (1 + sc[:, None]) + shift[:, None]
        x_norm = modulate(_ln(x), shift_a, scale_a)
        qkv = x_norm @ W_qkv + b_qkv
        q, k, v = jnp.split(qkv, 3, axis=-1)
        q = q.reshape(B, N, NH, hd).transpose(0, 2, 1, 3)
        k = k.reshape(B, N, NH, hd).transpose(0, 2, 1, 3)
        v = v.reshape(B, N, NH, hd).transpose(0, 2, 1, 3)
        attn_w = jax.nn.softmax(jnp.einsum('bhqd,bhkd->bhqk', q, k) * scale, axis=-1)
        attn_out = jnp.einsum('bhqk,bhkd->bhqd', attn_w, v)
        attn_out = attn_out.transpose(0, 2, 1, 3).reshape(B, N, H)
        attn_out = attn_out @ W_proj + b_proj
        x = x + gate_a[:, None] * attn_out
        S = context.shape[1]
        q_c = _ln(x) @ W_qc + b_qc
        kv_c = _ln(context) @ W_kvc + b_kvc
        k_c, v_c = jnp.split(kv_c, 2, axis=-1)
        q_c = q_c.reshape(B, N, NH, hd).transpose(0, 2, 1, 3)
        k_c = k_c.reshape(B, S, NH, hd).transpose(0, 2, 1, 3)
        v_c = v_c.reshape(B, S, NH, hd).transpose(0, 2, 1, 3)
        c_attn_w = jax.nn.softmax(jnp.einsum('bhqd,bhsd->bhqs', q_c, k_c) * scale, axis=-1)
        c_attn_out = jnp.einsum('bhqs,bhsd->bhqd', c_attn_w, v_c)
        c_attn_out = c_attn_out.transpose(0, 2, 1, 3).reshape(B, N, H)
        c_attn_out = c_attn_out @ W_cproj + b_cproj
        x = x + c_attn_out
        x_norm2 = modulate(_ln(x), shift_m, scale_m)
        h = jax.nn.gelu(x_norm2 @ W_mlp1 + b_mlp1)
        h = h @ W_mlp2 + b_mlp2
        x = x + gate_m[:, None] * h
        return x

    def _L1_xcond_ref(x, noise_emb, context, ln1_w, ln1_b, ln2_w, ln2_b, ln3_w, ln3_b, qkv_w, sa_out_w, q_w, k_w, v_w, ca_out_w, ffn_w1, ffn_b1, ffn_w2, ffn_b2):
        import jax, jax.numpy as jnp
        import numpy as np
        import math
        D_MODEL = 256
        N_HEADS = 16
        HEAD_DIM = D_MODEL // N_HEADS
        D_FF = 1024
        EPS = 1e-05
        ROPE_BASE = 10000.0

        def _rope(t):
            L, Dh = (t.shape[1], t.shape[-1])
            half = Dh // 2
            inv_freq = 1.0 / ROPE_BASE ** (jnp.arange(half, dtype=t.dtype) / half)
            ang = jnp.arange(L, dtype=t.dtype)[:, None] * inv_freq[None, :]
            cos = jnp.cos(ang)[None, :, None, :]
            sin = jnp.sin(ang)[None, :, None, :]
            t1, t2 = (t[..., :half], t[..., half:])
            return jnp.concatenate([t1 * cos - t2 * sin, t2 * cos + t1 * sin], axis=-1)

        def _adaln(x, emb, w, b):
            e = emb[:, 0, :]
            gb = e @ w.T + b
            gamma, beta = jnp.split(gb, 2, axis=-1)
            mu = x.mean(-1, keepdims=True)
            var = x.var(-1, keepdims=True)
            xn = (x - mu) * jax.lax.rsqrt(var + EPS)
            return xn * (1.0 + gamma[:, None, :]) + beta[:, None, :]

        def _attn(q, k, v):
            scale = 1.0 / math.sqrt(HEAD_DIM)
            scores = jnp.einsum('bqhd,bkhd->bhqk', q, k) * scale
            w = jax.nn.softmax(scores, axis=-1)
            out = jnp.einsum('bhqk,bkhd->bqhd', w, v)
            B, Lq = (out.shape[0], out.shape[1])
            return out.reshape(B, Lq, D_MODEL)
        B, L, D = x.shape
        L_ctx = context.shape[1]
        res = x
        xn = _adaln(x, noise_emb, ln1_w, ln1_b)
        qkv = xn @ qkv_w.T
        q, k, v = jnp.split(qkv, 3, axis=-1)
        q = _rope(q.reshape(B, L, N_HEADS, HEAD_DIM))
        k = _rope(k.reshape(B, L, N_HEADS, HEAD_DIM))
        v = v.reshape(B, L, N_HEADS, HEAD_DIM)
        sa = _attn(q, k, v) @ sa_out_w.T
        x = res + sa
        res = x
        xn = _adaln(x, noise_emb, ln2_w, ln2_b)
        q = _rope((xn @ q_w.T).reshape(B, L, N_HEADS, HEAD_DIM))
        k = _rope((context @ k_w.T).reshape(B, L_ctx, N_HEADS, HEAD_DIM))
        v = (context @ v_w.T).reshape(B, L_ctx, N_HEADS, HEAD_DIM)
        ca = _attn(q, k, v) @ ca_out_w.T
        x = res + ca
        res = x
        xn = _adaln(x, noise_emb, ln3_w, ln3_b)
        h = jax.nn.gelu(xn @ ffn_w1.T + ffn_b1, approximate=False)
        x = res + (h @ ffn_w2.T + ffn_b2)
        return x
    x = _L0_xcond_ref(x, cond_1024, ctx_1024, L0_xcond_W_mod, L0_xcond_b_mod, L0_xcond_W_qkv, L0_xcond_b_qkv, L0_xcond_W_proj, L0_xcond_b_proj, L0_xcond_W_qc, L0_xcond_b_qc, L0_xcond_W_kvc, L0_xcond_b_kvc, L0_xcond_W_cproj, L0_xcond_b_cproj, L0_xcond_W_mlp1, L0_xcond_b_mlp1, L0_xcond_W_mlp2, L0_xcond_b_mlp2)
    x = _L1_xcond_ref(x, cond_1024[:, None, :], ctx_1024, L1_xcond_ln1_w, L1_xcond_ln1_b, L1_xcond_ln2_w, L1_xcond_ln2_b, L1_xcond_ln3_w, L1_xcond_ln3_b, L1_xcond_qkv_w, L1_xcond_sa_out_w, L1_xcond_q_w, L1_xcond_k_w, L1_xcond_v_w, L1_xcond_ca_out_w, L1_xcond_ffn_w1, L1_xcond_ffn_b1, L1_xcond_ffn_w2, L1_xcond_ffn_b2)
    return x

_drawn_inputs = setup_inputs


def setup_inputs(seed=0):
    import zlib

    import numpy as np

    out = dict(_drawn_inputs(seed))
    spreads = {'L0_xcond_b_mod': (0.0, 0.1),
     'L0_xcond_b_qkv': (0.0, 0.1),
     'L0_xcond_b_proj': (0.0, 0.1),
     'L0_xcond_b_qc': (0.0, 0.531),
     'L0_xcond_b_kvc': (0.0, 0.1),
     'L0_xcond_b_cproj': (0.0, 0.1),
     'L0_xcond_b_mlp1': (0.0, 0.1),
     'L0_xcond_b_mlp2': (0.0, 0.1)}
    factors = {'L1_xcond_ln1_b': 34.558,
     'L1_xcond_ln2_w': 8.0,
     'L1_xcond_ln2_b': 26.478,
     'L1_xcond_ln3_b': 23.726,
     'L1_xcond_q_w': 8.0,
     'L1_xcond_k_w': 8.0,
     'L1_xcond_ffn_b1': 8.0,
     'L1_xcond_ffn_b2': 3.863}
    for name, (base, spread) in spreads.items():
        noise = np.random.default_rng([zlib.crc32(name.encode()), seed]).standard_normal(out[name].shape)
        drawn = base * np.exp(spread * noise) if base else spread * noise
        out[name] = jnp.asarray(drawn.astype(out[name].dtype))
    for name, factor in factors.items():
        out[name] = (out[name] * factor).astype(out[name].dtype)
    return out
```

```python
from contextlib import ExitStack

import numpy as np
import concourse.bass as bass
from concourse import mybir

F32 = mybir.dt.float32
BF16 = mybir.dt.bfloat16
ALU = mybir.AluOpType
ACT = mybir.ActivationFunctionType
AX = mybir.AxisListType

P = 128
B, N, D, NH = 8, 256, 256, 16
HD = D // NH
S = 77
F = 1024
KT = D // P
NT = N // P
FT = F // P
STREAMS = 2
ITERS = B // STREAMS
LAYERS = 2
SITES = 3
SCALE = HD ** -0.5
EPS = (1e-6, 1e-5)
HEADS_A_TILE = P // HD
QUAD = 4
PAIR = 2 * HD
DROWS = PAIR // (2 * (D // P))
NORM_SITES = 5
TERMS = [(0, 0), (0, 1), (1, 0), (1, 1), (0, 2), (2, 0)]
TROWS = HD * len(TERMS)
MROWS = TROWS + 2
SELF, CROSS = 0, 1
AHEAD = 1

NORM_COL = {(0, 0): 0, (0, 2): 1, (1, 0): 2, (1, 1): 3, (1, 2): 4}
PRE = {(0, 0): 0, (0, 1): 1, (0, 2): 2, (1, 2): 3}


def site(l, i):
    return l * SITES + i


def plan():
    A, Z = 0, 1
    order = []

    def scores(s, l, c):
        return [("scores", s, l, c, j) for j in range(NH if c == SELF else NH // 2)]

    def attend(s, l, c):
        quads = NH // QUAD
        out = [("probs", s, l, c, 0)]
        for g in range(1, quads):
            out += [("probs", s, l, c, g), ("pv", s, l, c, g - 1)]
        return out + [("pv", s, l, c, quads - 1), ("norm", s, l, c)]

    def weave(a, b):
        if not b:
            return a
        out, at = [], 0
        for n, x in enumerate(a):
            out.append(x)
            until = (n + 1) * len(b) // len(a)
            out += b[at:until]
            at = until
        return out

    for s in (A, Z):
        order.append(("load", s))
    order.append(("context",))
    for s in (A, Z):
        order.append(("ln", s, 0, 0))
    order.append(("ctx_t",))
    order.append(("ctx_k", 0))
    order.append(("ctx_v", 0))
    for l in range(LAYERS):
        for s in (A, Z):
            if l:
                order.append(("ln", s, l, 0))
            order.append(("qkv", s, l))
        if l == 0:
            order.append(("ctx_k", 1))
            order.append(("ctx_v", 1))
        order += scores(A, l, SELF)
        order.append(("maxima", A, l, SELF))
        order += weave(scores(Z, l, SELF), attend(A, l, SELF))
        order.append(("maxima", Z, l, SELF))
        order.append(("proj", A, l, SELF))
        order.append(("ln", A, l, 1))
        order.append(("qc", A, l))
        order += weave(attend(Z, l, SELF), scores(A, l, CROSS))
        order.append(("maxima", A, l, CROSS))
        order.append(("proj", Z, l, SELF))
        order.append(("ln", Z, l, 1))
        order.append(("qc", Z, l))
        order += weave(attend(A, l, CROSS), scores(Z, l, CROSS))
        order.append(("maxima", Z, l, CROSS))
        order.append(("proj", A, l, CROSS))
        order.append(("ln", A, l, 2))
        order += attend(Z, l, CROSS)
        order.append(("proj", Z, l, CROSS))
        order.append(("ln", Z, l, 2))
        for s in (A, Z):
            order += [("up", s, l, j) for j in range(FT // 2)]
        for s in (A, Z):
            order.append(("down", s, l))
    for s in (A, Z):
        order.append(("store", s))
    return order


PLAN = plan()

WORK, MAXB, PROB, OUTB, DENB = (0, 1), (2, 3), (4, 5), (6,), (7,)


class Uses:

    def __init__(self):
        self.of, self.per, self.turn = {}, {}, {}

    def give(self, pool, key):
        t = self.turn.get(pool, 0)
        self.turn[pool] = t + 1
        b = pool[t % len(pool)]
        n = self.per.get(b, 0)
        self.per[b] = n + 1
        self.of[key] = (b, n)


def assign():
    banks, probs = Uses(), Uses()
    for st in PLAN:
        name = st[0]
        if name in ("ln", "ctx_t", "qc", "proj", "down", "up", "maxima", "ctx_v", "ctx_k"):
            banks.give(WORK, st)
        elif name == "qkv":
            for part in "qkv":
                banks.give(WORK, (*st, part))
        elif name == "scores":
            banks.give(MAXB, st)
        elif name == "probs":
            for u in range(QUAD if st[3] == SELF else QUAD // 2):
                banks.give(PROB, (*st, u))
            probs.give((0, 1), st[1:])
        elif name == "pv" and st[4] == 0:
            banks.give(OUTB, ("out", *st[1:4]))
            banks.give(DENB, ("den", *st[1:4]))
    return banks, probs


BANKS, PROBS = assign()


def head_of(g, t):
    half, ab = g // 2, g % 2
    return half * HEADS_A_TILE + 2 * t + ab, half, half * QUAD + t, ab


def slot(h):
    return (h % HEADS_A_TILE) * KT + h // HEADS_A_TILE


def build(nc, ins, out):
    with ExitStack() as ctx:
        def sb(name, shape, dt=F32):
            return ctx.enter_context(nc.sbuf_tensor(name, shape, dt))

        def sem(name):
            return ctx.enter_context(nc.semaphore(name))

        def both(name):
            return [sem(f"{name}{s}") for s in range(STREAMS)]

        w_qkv = [sb(f"w_qkv{l}", [P, KT, 3 * D]) for l in range(LAYERS)]
        w_proj = [[sb(f"w_proj{l}{c}", [P, KT, D]) for c in range(2)] for l in range(LAYERS)]
        w_qc = [sb(f"w_qc{l}", [P, KT, D]) for l in range(LAYERS)]
        w_kvc = [sb(f"w_kvc{l}", [P, KT, 2 * D]) for l in range(LAYERS)]
        w_up = [sb(f"w_up{l}", [P, KT, F]) for l in range(LAYERS)]
        w_down = [sb(f"w_down{l}", [P, FT, D]) for l in range(LAYERS)]
        ident = sb("ident", [P, P])
        identb = sb("identb", [P, P], BF16)
        cos = sb("cos", [P, N])
        sin = sb("sin", [P, N])
        b_v = sb("b_v", [P, D])
        b_cproj = sb("b_cproj", [P, D])
        b_vc = sb("b_vc", [S, D])
        b_ffn = sb("b_ffn", [P, D])
        b_qk = sb("b_qk", [P, 2 * KT])
        b_qc = sb("b_qc", [P, KT])
        b_kc = sb("b_kc", [P, KT])
        b_up = [sb(f"b_up{l}", [P, FT]) for l in range(LAYERS)]
        ones = sb("ones", [P, 4, PAIR])
        minus_half = sb("minus_half", [P, NT])
        eps_tile = sb("eps_tile", [P, LAYERS, NT])
        spare = sb("spare", [P, 2])
        mod_all = sb("mod_all", [P, NORM_SITES * 2 * KT, B])
        silu = sb("silu", [P, 4, KT, B])
        per = range(STREAMS)
        x = [sb(f"x{s}", [P, NT, D]) for s in per]
        xhat = [sb(f"xhat{s}", [P, NT, D]) for s in per]
        rden = [xhat[s][:].rearrange("p t d -> p (t d)") for s in per]
        xT = [sb(f"xT{s}", [P, KT, N]) for s in per]
        hT = [sb(f"hT{s}", [P, FT, N]) for s in per]
        qk = [hT[s][:, 0:4, :] for s in per]
        rot = [hT[s][:, 4:8, :] for s in per]
        parts = [sb(f"parts{s}", [P, 3, 4, N], BF16) for s in per]
        stack = [sb(f"stack{s}", [P, 2, NH, N], BF16) for s in per]
        v = [sb(f"v{s}", [P, NT, NH // 2, 2 * PAIR]) for s in per]
        gates = [sb(f"gates{s}", [P, 4, D]) for s in per]
        mod = [sb(f"mod{s}", [P, NORM_SITES * 2 * KT]) for s in per]
        kc_stack = [[sb(f"kc_stack{l}{s}", [MROWS, NH, S], BF16) for s in per] for l in range(LAYERS)]
        vc = [[sb(f"vc{l}{s}", [S, NH // 2, 2 * PAIR]) for s in per] for l in range(LAYERS)]
        stats = [sb(f"stats{s}", [P, NT, 6]) for s in per]
        mv = [sb(f"mv{s}", [P, NT, 2]) for s in per]
        rstd = [sb(f"rstd{s}", [P, 2, NT]) for s in per]
        nmax = [sb(f"nmax{s}", [P, NT, NH]) for s in per]
        nparts = [sb(f"nparts{s}", [P, NT, 2, NH], BF16) for s in per]
        nT = [sb(f"nT{s}", [2 * NH, N], BF16) for s in per]
        probs = sb("probs", [P, 2, QUAD, NT * N])
        ctx_in = sb("ctx_in", [S, STREAMS, D])
        ctx_hat = sb("ctx_hat", [S, STREAMS, D])
        ctx_T = [sb(f"ctx_T{l}", [P, KT, STREAMS, S]) for l in range(LAYERS)]
        kc = sb("kc", [P, STREAMS, KT, S])
        kc_rot = sb("kc_rot", [P, STREAMS, KT, S])
        kc_parts = sb("kc_parts", [P, 3, STREAMS, KT, S], BF16)
        c_stats = sb("c_stats", [S, STREAMS, 6])
        c_mv = sb("c_mv", [S, STREAMS, 2])
        c_rstd = sb("c_rstd", [S, 2, STREAMS])
        w_mod = probs[:].rearrange("p a b c -> p (a b c)")[:, 0:KT * 6 * D].rearrange("p (k n) -> p k n", k=KT)
        w_ln = stack[0][:].rearrange("p a b c -> p (a b c)").bitcast(F32)[:, 0:KT * 6 * D].rearrange("p (k n) -> p k n", k=KT)
        c_rows = stack[1][:].rearrange("p a b c -> p (a b c)").bitcast(F32)[0:B, 0:12 * D]
        c_bias = hT[0][:].rearrange("p a b -> p (a b)")[0:B, 0:6 * D]
        c_bias1 = hT[1][:].rearrange("p a b -> p (a b)")[0:B, 0:6 * D]
        g_bias = parts[0][:].rearrange("p a b c -> p (a b c)").bitcast(F32)[0:B, 0:2 * D]
        g_rows = parts[1][:].rearrange("p a b c -> p (a b c)").bitcast(F32)[0:B, 0:4 * D]

        psum = ctx.enter_context(nc.psum_tensor("psum", [P, 8, 512], F32))
        qk_dram = [nc.dram_tensor(f"qk_dram{s}", [P, 3, 4 * N], BF16).ap() for s in per]
        kc_dram = nc.dram_tensor("kc_dram", [P, 3, STREAMS * KT * S], BF16).ap()
        g_dram = nc.dram_tensor("gates_dram", [B, 4 * D], F32).ap()

        bank_full = [sem(f"bank_full{b}") for b in range(8)]
        bank_read = [sem(f"bank_read{b}") for b in range(8)]
        probs_used = [sem(f"probs_used{b}") for b in range(2)]
        x_loaded, gates_loaded, stored = both("x_loaded"), both("gates_loaded"), both("stored")
        x_added, x_biased, mod_ready = both("x_added"), both("x_biased"), both("mod_ready")
        stats_done, mv_ready, var_eps, rstd_ready, xhat_ready = (
            both("stats_done"), both("mv_ready"), both("var_eps"), both("rstd_ready"), both("xhat_ready"))
        rope_rot, rope_cos, rope_sin, rope_done = both("rope_rot"), both("rope_cos"), both("rope_sin"), both("rope_done")
        parts_ready, rest_ready, stacked, rden_ready = both("parts_ready"), both("rest_ready"), both("stacked"), both("rden_ready")
        nmax_done, nhigh_done, nparts_ready, n_stacked = (
            both("nmax_done"), both("nhigh_done"), both("nparts_ready"), both("n_stacked"))
        ctx_loaded, ctxT_loaded = sem("ctx_loaded"), sem("ctxT_loaded")
        c_stats_done, c_mv_ready, c_var_eps, c_rstd_ready, ctx_hat_ready = (
            sem("c_stats_done"), sem("c_mv_ready"), sem("c_var_eps"), sem("c_rstd_ready"), sem("ctx_hat_ready"))
        kc_rotated, kc_cos, kc_sin, kc_roped, kc_parts_ready, kc_rest, kc_stacked = (
            sem("kc_rotated"), sem("kc_cos"), sem("kc_sin"), sem("kc_roped"), sem("kc_parts_ready"),
            sem("kc_rest"), sem("kc_stacked"))
        written = [[sem(f"written{s}{p}") for p in range(3)] for s in per]
        kc_written = [sem(f"kc_written{p}") for p in range(3)]
        mod_loads, w_loads = sem("mod_loads"), sem("w_loads")
        pro_exp, pro_dve, pro_pe, pro_free, pro_gates = (
            sem("pro_exp"), sem("pro_dve"), sem("pro_pe"), sem("pro_free"), sem("pro_gates"))
        identb_ready = sem("identb_ready")
        zeros_ready, consts_ready, mod_all_ready, stack_ones = sem("zeros_ready"), sem("consts_ready"), sem("mod_all_ready"), sem("stack_ones")

        def full(eng, it, key):
            b, n = BANKS.of[key]
            eng.wait_ge(bank_full[b], it * BANKS.per[b] + n + 1)
            return psum[:, b, :]

        def free(eng, it, key):
            b, n = BANKS.of[key]
            eng.wait_ge(bank_read[b], it * BANKS.per[b] + n + AHEAD)
            return psum[:, b, :]

        def fills(ins_, key):
            ins_.then_inc(bank_full[BANKS.of[key][0]], 1)

        def reads(ins_, key):
            ins_.then_inc(bank_read[BANKS.of[key][0]], 1)

        def brought(eng, it, key):
            b, n = BANKS.of[key]
            eng.wait_ge(bank_read[b], it * BANKS.per[b] + n + 1 + AHEAD)

        def carry_wait():
            nc.vector.tensor_copy(spare[:, 1:2], spare[:, 0:1])

        def event(l, c):
            return l * 2 + c

        def cols(ap):
            return ap.rearrange("(k p) n -> p k n", p=P)

        small = [
            (ident[:], ins["ident"]), (cos[:], ins["cos"]), (sin[:], ins["sin"]),
            (b_v[:], ins["b_qkv0"][2 * D:3 * D].partition_broadcast(P)),
            (b_cproj[:], ins["b_cproj0"][0:D].partition_broadcast(P)),
            (b_vc[:], ins["b_kvc0"][D:2 * D].partition_broadcast(S)),
            (b_ffn[:], ins["b_down1"][0:D].partition_broadcast(P)),
            (b_qk[:], ins["b_qk_cols"]), (b_qc[:], ins["b_qc_cols"]), (b_kc[:], ins["b_kc_cols"]),
            (b_up[0][:], ins["b_up0_cols"]), (b_up[1][:], ins["b_up1_cols"]),
        ]
        big = []
        for l in range(LAYERS):
            big += [(w_qkv[l][:], cols(ins[f"w_qkv{l}"])), (w_kvc[l][:], cols(ins[f"w_kvc{l}"])),
                    (w_qc[l][:], cols(ins[f"w_qc{l}"])), (w_proj[l][0][:], cols(ins[f"w_proj{l}"])),
                    (w_proj[l][1][:], cols(ins[f"w_cproj{l}"])), (w_up[l][:], cols(ins[f"w_up{l}"])),
                    (w_down[l][:], cols(ins[f"w_down{l}"]))]
        first = [(silu[:, 0, :, :], ins["condT"].rearrange("(k p) b -> p k b", p=P)),
                 (w_mod, cols(ins["w_mod0"])), (c_bias, ins["b_mod0"][0:6 * D].partition_broadcast(B)),
                 (g_bias[:, 0:D], ins["b_proj0"][0:D].partition_broadcast(B)),
                 (g_bias[:, D:2 * D], ins["b_down0"][0:D].partition_broadcast(B))]
        for i in range(SITES):
            first.append((w_ln[:, :, i * 2 * D:(i + 1) * 2 * D], cols(ins[f"w_ln{i}"])))
            first.append((c_bias1[:, i * 2 * D:(i + 1) * 2 * D], ins[f"b_ln{i}"][0:2 * D].partition_broadcast(B)))
        MOD_CHUNKS = 6

        block = ctx.enter_context(nc.Block())

        @block.sync
        def _(sp):
            for dst, src in first:
                sp.dma_start(dst, src).then_inc(mod_loads, 16)
            for dst, src in small + big:
                sp.dma_start(dst, src).then_inc(w_loads, 16)
            sp.wait_ge(pro_gates, 1)
            sp.dma_start(g_dram, g_rows).then_inc(pro_free, 16)
            sp.wait_ge(pro_free, 16)
            sp.wait_ge(stack_ones, 1)

            with sp.Fori(0, ITERS) as it:
                def load(s):
                    sp.wait_ge(stored[s], (it + AHEAD) * 16)
                    sp.dma_start(x[s][:], ins["x"][it * STREAMS + s].rearrange("(t p) d -> p t d", p=P)).then_inc(x_loaded[s], 16)
                    sp.dma_start(gates[s][:], g_dram[it * STREAMS + s].partition_broadcast(P)).then_inc(gates_loaded[s], 16)

                def context():
                    for s in per:
                        sp.wait_ge(x_added[s], it * LAYERS * SITES + AHEAD)
                    for s in per:
                        sp.dma_start(ctx_in[:, s, :], ins["ctx"][it * STREAMS + s]).then_inc(ctx_loaded, 16)
                        sp.dma_start(ctx_T[1][:, :, s, :], ins["ctxT"][it * STREAMS + s].rearrange("(k p) n -> p k n", p=P)).then_inc(ctxT_loaded, 16)

                def through_dram(src, dram, ready, base, written, before, gather):
                    for part in range(3):
                        sp.wait_ge(ready, base + part + 1)
                        sp.dma_start(dram[:, part], src[:, part]).then_inc(written[part], 16)
                    for part in range(3):
                        sp.wait_ge(written[part], (before + 1) * 16)
                        gather(part)

                def by_head(dram, part, at, w):
                    row = dram.ap[0][0]
                    return bass.AP(dram.tensor, dram.offset + part * dram.ap[1][0] + at, [[row, HD], [HD * row, HEADS_A_TILE], [1, w]])

                def stack_q(s, l, c):
                    e = event(l, c)
                    n = 4 if c == SELF else 2

                    def gather(part):
                        for t, term in enumerate(TERMS):
                            for side in range(2 if c == SELF else 1):
                                if term[side] == part:
                                    dst = stack[s][t * HD:(t + 1) * HD, side].rearrange("d (h m) n -> d h (m n)", m=KT)
                                    sp.dma_start(dst, by_head(qk_dram[s], part, side * KT * N, KT * N)).then_inc(stacked[s], 16)

                    through_dram(parts[s][:, :, 0:n, :].rearrange("p a m n -> p a (m n)"), qk_dram[s][:, :, 0:n * N],
                                 parts_ready[s], it * 12 + 3 * e, written[s], it * 4 + e, gather)

                def stack_kc(l):
                    def gather(part):
                        for t, term in enumerate(TERMS):
                            if term[1] == part:
                                for s in per:
                                    dst = kc_stack[l][s][t * HD:(t + 1) * HD].rearrange("d (h m) n -> d h (m n)", m=KT)
                                    sp.dma_start(dst, by_head(kc_dram, part, s * KT * S, KT * S)).then_inc(kc_stacked, 16)

                    through_dram(kc_parts[:].rearrange("p a s k n -> p a (s k n)"), kc_dram, kc_parts_ready, it * 6 + 3 * l + AHEAD,
                                 kc_written, it * LAYERS + l, gather)

                def stack_maxima(s, l, c):
                    brought(sp, it, ("maxima", s, l, c))
                    for part in range(2):
                        sp.dma_start(stack[s][TROWS + part:TROWS + part + 1, 0, :, :], nT[s][part * NH:(part + 1) * NH, :]).then_inc(n_stacked[s], 16)

                def store(s):
                    sp.wait_ge(x_added[s], (it + 1) * LAYERS * SITES + AHEAD)
                    sp.dma_start(out[it * STREAMS + s].rearrange("(t p) d -> p t d", p=P), x[s][:]).then_inc(stored[s], 16)

                for st in PLAN:
                    if st[0] == "load":
                        load(st[1])
                    elif st[0] == "context":
                        context()
                    elif st[0] == "qkv":
                        stack_q(st[1], st[2], SELF)
                    elif st[0] == "qc":
                        stack_q(st[1], st[2], CROSS)
                    elif st[0] == "ctx_k":
                        stack_kc(st[1])
                    elif st[0] == "maxima":
                        stack_maxima(*st[1:])
                    elif st[0] == "store":
                        store(st[1])
            for s in per:
                sp.wait_ge(stored[s], (ITERS + AHEAD) * 16)

        @block.gpsimd
        def _(pool):
            g = nc.gpsimd
            pool.wait_ge(w_loads, 16 * len(small + big))
            pool.wait_ge(consts_ready, 1)
            pool.wait_ge(mod_all_ready, 1)
            with pool.Fori(0, ITERS) as it:
                def load(s):
                    pool.wait_ge(x_added[s], it * LAYERS * SITES + AHEAD)
                    g.tensor_copy(mod[s][:], mod_all[:, :, it * STREAMS + s]).then_inc(mod_ready[s], 1)

                def inv_std(mv_, r, ready, eps_done, done, e, per_it, eps, n):
                    pool.wait_ge(ready, it * per_it + e + 1)
                    g.tensor_tensor(r[:, 0, :], mv_[:, :, 1], eps, ALU.add).then_inc(eps_done, 1)
                    pool.wait_ge(eps_done, it * per_it + e + 1)
                    g.tensor_tensor(r[:, 1, :], r[:, 0, :], minus_half[0:n, :], ALU.pow).then_inc(done, 1)

                def ln(s, l, i):
                    e = site(l, i)
                    inv_std(mv[s], rstd[s], mv_ready[s], var_eps[s], rstd_ready[s], e, LAYERS * SITES, eps_tile[:, l, :], P)
                    if (l, i) in PRE:
                        pool.wait_ge(xhat_ready[s], it * LAYERS * SITES + e + 1)
                        if (l, i) == (0, 0):
                            pool.wait_ge(gates_loaded[s], (it + 1) * 16)
                        bias = {(0, 0): gates[s][:, 1, :], (0, 1): b_cproj[:], (0, 2): gates[s][:, 3, :], (1, 2): b_ffn[:]}[(l, i)]
                        for t in range(NT):
                            last = g.tensor_tensor(x[s][:, t, :], x[s][:, t, :], bias, ALU.add)
                        last.then_inc(x_biased[s], 1)

                def rope(s, l, c):
                    if l == 1:
                        n = 4 if c == SELF else 2
                        pool.wait_ge(rope_rot[s], it * 2 + c + 1)
                        for m in range(n):
                            last = g.tensor_tensor(qk[s][:, m, :], qk[s][:, m, :], cos[:], ALU.mult)
                        last.then_inc(rope_cos[s], 1)

                for st in PLAN:
                    if st[0] == "load":
                        load(st[1])
                    elif st[0] == "context":
                        inv_std(c_mv, c_rstd, c_mv_ready, c_var_eps, c_rstd_ready, 0, 1, eps_tile[0:S, 0, :], S)
                    elif st[0] == "ln":
                        ln(*st[1:])
                    elif st[0] == "qkv":
                        rope(st[1], st[2], SELF)
                    elif st[0] == "qc":
                        rope(st[1], st[2], CROSS)

        @block.scalar
        def _(act):
            a = nc.scalar
            act.wait_ge(mod_loads, 16 * len(first))
            a.activation(silu[:, 1], silu[:, 0], ACT.Exp, scale=-1.0).then_inc(pro_exp, 1)
            act.wait_ge(w_loads, 16 * len(small + big))
            with act.Fori(0, ITERS) as it:
                def ln(s, l, i):
                    ps = full(act, it, ("ln", s, l, i))
                    if (l, i) == (0, 0):
                        act.wait_ge(mod_ready[s], it + 1)
                    if (l, i) in NORM_COL:
                        col = NORM_COL[(l, i)] * 2 * KT
                        for k in range(KT):
                            last = a.activation(xT[s][:, k, :], ps[:, k * N:(k + 1) * N], ACT.Identity,
                                                scale=mod[s][:, col + k:col + k + 1],
                                                bias=mod[s][:, col + KT + k:col + KT + k + 1])
                    else:
                        last = a.activation(xT[s][:].rearrange("p k n -> p (k n)"), ps, ACT.Copy)
                    reads(last, ("ln", s, l, i))

                def q_out(s, l, c):
                    for part in ("q", "k") if c == SELF else ("q",):
                        key = ("qkv", s, l, part) if c == SELF else ("qc", s, l)
                        ps = full(act, it, key)
                        m0 = 0 if part == "q" else KT
                        if l == 0:
                            bias = b_qk if c == SELF else b_qc
                            for m in range(KT):
                                last = a.activation(qk[s][:, m0 + m, :], ps[:, m * N:(m + 1) * N], ACT.Identity,
                                                    bias=bias[:, m0 + m:m0 + m + 1])
                        else:
                            last = a.activation(qk[s][:, m0:m0 + KT, :].rearrange("p m n -> p (m n)"), ps, ACT.Copy)
                        reads(last, key)

                def ctx_t():
                    ps = full(act, it, ("ctx_t",))
                    reads(a.activation(ctx_T[0][:].rearrange("p k s n -> p (k s n)"), ps[:, 0:KT * STREAMS * S], ACT.Copy), ("ctx_t",))

                def kc_out(l):
                    ps = full(act, it, ("ctx_k", l))
                    act.wait_ge(kc_parts_ready, it * 6 + l * 3 + AHEAD)
                    for m in range(KT):
                        src = ps[:, m * STREAMS * S:(m + 1) * STREAMS * S].rearrange("p (s n) -> p s n", s=STREAMS)
                        if l == 0:
                            last = a.activation(kc[:, :, m, :], src, ACT.Identity, bias=b_kc[:, m:m + 1])
                        else:
                            last = a.activation(kc[:, :, m, :], src, ACT.Copy)
                    reads(last, ("ctx_k", l))

                def maxima(s, l, c):
                    ps = full(act, it, ("maxima", s, l, c))
                    src = ps[0:2 * NH, 0:N // 2].bitcast(BF16)
                    reads(a.activation(nT[s][:], src, ACT.Copy), ("maxima", s, l, c))

                def exps(s, l, c, g):
                    buf, n = PROBS.of[(s, l, c, g)]
                    act.wait_ge(probs_used[buf], it * PROBS.per[buf] + n + AHEAD)
                    for u in range(QUAD if c == SELF else QUAD // 2):
                        key = ("probs", s, l, c, g, u)
                        ps = full(act, it, key)
                        if c == SELF:
                            last = a.activation(probs[:, buf, u, :], ps, ACT.Exp, scale=SCALE)
                        else:
                            last = a.activation(probs[0:S, buf, 2 * u:2 * u + 2, 0:N],
                                                ps[0:S, :].rearrange("p (h n) -> p h n", h=2), ACT.Exp, scale=SCALE)
                        reads(last, key)

                def gelu(s, l, j):
                    ps = full(act, it, ("up", s, l, j))
                    fn = ACT.Gelu_apprx_tanh if l == 0 else ACT.Gelu
                    for m in range(2):
                        f = 2 * j + m
                        last = a.activation(hT[s][:, f, :], ps[:, m * N:(m + 1) * N], fn, bias=b_up[l][:, f:f + 1])
                    reads(last, ("up", s, l, j))

                for st in PLAN:
                    if st[0] == "ln":
                        ln(*st[1:])
                    elif st[0] == "qkv":
                        q_out(st[1], st[2], SELF)
                    elif st[0] == "qc":
                        q_out(st[1], st[2], CROSS)
                    elif st[0] == "ctx_t":
                        ctx_t()
                    elif st[0] == "ctx_k":
                        kc_out(st[1])
                    elif st[0] == "maxima":
                        maxima(*st[1:])
                    elif st[0] == "probs":
                        exps(*st[1:])
                    elif st[0] == "up":
                        gelu(*st[1:])

        @block.vector
        def _(dve):
            d = nc.vector
            d.memset(ones[:], 0.0).then_inc(zeros_ready, 1)
            d.memset(minus_half[:], -0.5)
            d.memset(spare[:], 0.0)
            for l in range(LAYERS):
                d.memset(eps_tile[:, l], EPS[l])
            for s in per:
                d.memset(v[s][:], 0.0)
                for l in range(LAYERS):
                    d.memset(vc[l][s][:], 0.0)
                    d.memset(kc_stack[l][s][TROWS:MROWS], 1.0)
            for sem_ in bank_read + probs_used + x_added + [kc_parts_ready]:
                dve.sem_inc(sem_, AHEAD)
            for sem_ in stored + [kc_stacked]:
                dve.sem_inc(sem_, 16 * AHEAD)
            dve.wait_ge(zeros_ready, 1)
            for n in range(4):
                last = d.memset(ones[:, n, n * DROWS:(n + 1) * DROWS], 1.0)
            last.then_inc(consts_ready, 1)
            dve.wait_ge(pro_exp, 1)
            d.tensor_scalar(silu[:, 2], silu[:, 1], 1.0, None, ALU.add).then_inc(pro_dve, 1)
            dve.wait_ge(pro_dve, 1)
            d.reciprocal(silu[:, 1], silu[:, 2]).then_inc(pro_dve, 1)
            dve.wait_ge(pro_dve, 2)
            d.tensor_tensor(silu[:, 3], silu[:, 0], silu[:, 1], ALU.mult).then_inc(pro_dve, 1)
            bias_rows = [c_bias, c_bias1]
            for n in range(MOD_CHUNKS):
                dve.wait_ge(pro_pe, n + 1)
                bias = bias_rows[n // 3][:, (n % 3) * 512:(n % 3) * 512 + 512]
                d.tensor_tensor(c_rows[:, n * 512:(n + 1) * 512], psum[0:B, n, :], bias, ALU.add).then_inc(pro_dve, 1)
            dve.wait_ge(pro_dve, 3 + MOD_CHUNKS)
            gate_at = (2 * D, 5 * D)
            scale_at = (D, 4 * D, 6 * D, 8 * D, 10 * D)
            shift_at = (0, 3 * D, 7 * D, 9 * D, 11 * D)
            for at in scale_at:
                last = d.tensor_scalar(c_rows[:, at:at + D], c_rows[:, at:at + D], 1.0, None, ALU.add)
            last.then_inc(pro_dve, 1)
            for n, at in enumerate(gate_at):
                d.tensor_copy(g_rows[:, 2 * n * D:(2 * n + 1) * D], c_rows[:, at:at + D])
                last = d.tensor_tensor(g_rows[:, (2 * n + 1) * D:(2 * n + 2) * D], c_rows[:, at:at + D], g_bias[:, n * D:(n + 1) * D], ALU.mult)
            last.then_inc(pro_gates, 1)
            dve.wait_ge(pro_pe, MOD_CHUNKS + 1)
            d.tensor_copy(mod_all[:], psum[:, 7, 0:NORM_SITES * 2 * KT * B].rearrange("p (c b) -> p c b", b=B)).then_inc(mod_all_ready, 1)
            dve.wait_ge(pro_gates, 1)
            for s in per:
                last = d.memset(stack[s][TROWS:MROWS, 1], 1.0)
            last.then_inc(stack_ones, 1)
            dve.wait_ge(w_loads, 16 * len(small + big))
            d.tensor_copy(identb[:], ident[:]).then_inc(identb_ready, 1)
            dve.wait_ge(consts_ready, 1)
            with dve.Fori(0, ITERS) as it:
                def normalise(src, st_, mv_, r, dst, n, sems, e, per_it, eps_ready):
                    done, mvr, ready = sems
                    for t in range(2):
                        last = d.bn_stats(st_[:, t, :], src[:, t, :])
                    last.then_inc(done, 1)
                    dve.wait_ge(done, it * per_it + e + 1)
                    carry_wait()
                    for t in range(2):
                        last = d.bn_aggr(mv_[:, t, :], st_[:, t, :])
                    last.then_inc(mvr, 1)
                    dve.wait_ge(mvr, it * per_it + e + 1)
                    dve.wait_ge(eps_ready, it * per_it + e + 1)
                    for t in range(2):
                        last = d.tensor_scalar(dst[:, t, :], src[:, t, :], mv_[:, t, 0:1], r[:, 1, t:t + 1], ALU.subtract, ALU.mult)
                    last.then_inc(ready, 1)

                def ln(s, l, i):
                    e = site(l, i)
                    if e == 0:
                        dve.wait_ge(x_loaded[s], (it + 1) * 16)
                    else:
                        dve.wait_ge(x_added[s], it * LAYERS * SITES + e + AHEAD)
                    normalise(x[s], stats[s], mv[s], rstd[s], xhat[s], P, (stats_done[s], mv_ready[s], xhat_ready[s]),
                              e, LAYERS * SITES, rstd_ready[s])

                def context():
                    dve.wait_ge(ctx_loaded, (it + 1) * 16 * STREAMS)
                    normalise(ctx_in, c_stats, c_mv, c_rstd, ctx_hat, S, (c_stats_done, c_mv_ready, ctx_hat_ready), 0, 1, c_rstd_ready)

                def split(src, n, dst, rest_sem, ready, base_rest, base_ready):
                    d.tensor_copy(dst[0], src).then_inc(ready, 1)
                    dve.wait_ge(ready, base_ready + 1)
                    d.tensor_tensor(src, src, dst[0], ALU.subtract).then_inc(rest_sem, 1)
                    dve.wait_ge(rest_sem, base_rest + 1)
                    d.tensor_copy(dst[1], src).then_inc(ready, 1)
                    dve.wait_ge(ready, base_ready + 2)
                    d.tensor_tensor(dst[2], src, dst[1], ALU.subtract).then_inc(ready, 1)

                SWAP = [i ^ (HD // 2) for i in range(32)]

                def split_q(s, l, c):
                    n = 4 if c == SELF else 2
                    brought(dve, it, ("qkv", s, l, "k") if c == SELF else ("qc", s, l))
                    if l == 1:
                        carry_wait()
                    src = qk[s][:, 0:n, :]
                    if l == 1:
                        e = it * 2 + c + 1
                        turned = rot[s][:, 0:n, :]
                        d.stream_shuffle(turned, src, SWAP).then_inc(rope_rot[s], 1)
                        dve.wait_ge(rope_rot[s], e)
                        d.tensor_tensor(turned, turned, sin[:].unsqueeze(1).to_broadcast([P, n, N]), ALU.mult).then_inc(rope_sin[s], 1)
                        dve.wait_ge(rope_sin[s], e)
                        dve.wait_ge(rope_cos[s], e)
                        d.tensor_tensor(src, src, turned, ALU.add).then_inc(rope_done[s], 1)
                        dve.wait_ge(rope_done[s], e)
                    ev = event(l, c)
                    split(src, n, [parts[s][:, p, 0:n, :] for p in range(3)], rest_ready[s], parts_ready[s],
                          it * 4 + ev, it * 12 + 3 * ev)

                def v_out(ps, dst, bias, n):
                    to = bass.AP(dst.tensor, dst.offset, [dst.ap[0], [2 * PAIR, NH // 2], [PAIR + HD, 2], [1, HD]])
                    frm = ps.rearrange("p (h a d) -> p h a d", a=2, d=HD)
                    if bias is None:
                        return d.tensor_copy(to, frm)
                    return d.tensor_tensor(to, frm, bias.rearrange("p (h a d) -> p h a d", a=2, d=HD), ALU.add)

                def self_v(s, l):
                    key = ("qkv", s, l, "v")
                    ps = full(dve, it, key)
                    for t in range(NT):
                        last = v_out(ps[:, t * D:(t + 1) * D], v[s][:, t], b_v[:] if l == 0 else None, P)
                    reads(last, key)

                def ctx_v(l):
                    key = ("ctx_v", l)
                    ps = full(dve, it, key)
                    for s in per:
                        last = v_out(ps[0:S, s * D:(s + 1) * D], vc[l][s][:], b_vc[:] if l == 0 else None, S)
                    reads(last, key)

                def ctx_k(l):
                    brought(dve, it, ("ctx_k", l))
                    if l == 1:
                        carry_wait()
                    src = kc[:].rearrange("p s k n -> p (s k) n")
                    if l == 1:
                        turned = kc_rot[:].rearrange("p s k n -> p (s k) n")
                        wide = [P, STREAMS * KT, S]
                        d.stream_shuffle(turned, src, SWAP).then_inc(kc_rotated, 1)
                        dve.wait_ge(kc_rotated, it + 1)
                        d.tensor_tensor(turned, turned, sin[:, 0:S].unsqueeze(1).to_broadcast(wide), ALU.mult).then_inc(kc_sin, 1)
                        d.tensor_tensor(src, src, cos[:, 0:S].unsqueeze(1).to_broadcast(wide), ALU.mult).then_inc(kc_cos, 1)
                        dve.wait_ge(kc_sin, it + 1)
                        dve.wait_ge(kc_cos, it + 1)
                        d.tensor_tensor(src, src, turned, ALU.add).then_inc(kc_roped, 1)
                        dve.wait_ge(kc_roped, it + 1)
                    dve.wait_ge(kc_stacked, 16 * AHEAD + (it * LAYERS + l) * 16 * len(TERMS) * STREAMS)
                    split(src, None, [kc_parts[:, p].rearrange("p s k n -> p (s k) n") for p in range(3)], kc_rest, kc_parts_ready,
                          it * LAYERS + l, it * 6 + 3 * l + AHEAD)

                def row_max(s, l, c, j):
                    key = ("scores", s, l, c, j)
                    ps = full(dve, it, key)
                    if c == SELF:
                        last = d.tensor_reduce(nmax[s][:, :, slot(j)], ps.rearrange("p (t n) -> p t n", t=NT), AX.X, ALU.max, negate=True)
                    else:
                        for h in range(2):
                            src = ps[:, h * 2 * P:(h + 1) * 2 * P].rearrange("p (t n) -> p t n", t=NT)[:, :, 0:S]
                            last = d.tensor_reduce(nmax[s][:, :, slot(2 * j + h)], src, AX.X, ALU.max, negate=True)
                    reads(last, key)

                def maxima(s, l, c):
                    e = it * 4 + event(l, c) + 1
                    last_j = (NH if c == SELF else NH // 2) - 1
                    brought(dve, it, ("scores", s, l, c, last_j))
                    d.tensor_copy(nparts[s][:, :, 0, :], nmax[s][:]).then_inc(nhigh_done[s], 1)
                    dve.wait_ge(nhigh_done[s], e)
                    d.tensor_tensor(nparts[s][:, :, 1, :], nmax[s][:], nparts[s][:, :, 0, :], ALU.subtract).then_inc(nparts_ready[s], 1)

                def norm(s, l, c):
                    buf, n = PROBS.of[(s, l, c, NH // QUAD - 1)]
                    dve.wait_ge(probs_used[buf], it * PROBS.per[buf] + n + 1 + AHEAD)
                    inv = rot[s][:, 0, :]
                    reads(d.reciprocal(inv, psum[:, DENB[0], 0:N]), ("den", s, l, c))
                    brought(dve, it, ("den", s, l, c))
                    carry_wait()
                    for half in range(KT):
                        last = d.stream_shuffle(rden[s][:, half * N:(half + 1) * N], inv, [(half * 2 + i // HD) * DROWS for i in range(PAIR)])
                    last.then_inc(rden_ready[s], 1)
                    dve.wait_ge(rden_ready[s], it * 4 + event(l, c) + 1)
                    key = ("out", s, l, c)
                    reads(d.tensor_tensor(xT[s][:].rearrange("p k n -> p (k n)"), psum[:, OUTB[0], :], rden[s], ALU.mult), key)

                def residual(s, l, i, key):
                    ps = full(dve, it, key).rearrange("p (t n) -> p t n", t=NT)
                    if (l, i) in PRE:
                        dve.wait_ge(x_biased[s], it * len(PRE) + PRE[(l, i)] + 1)
                    if l == 0 and i != 1:
                        gate = gates[s][:, 0 if i == 0 else 2, :].unsqueeze(1).to_broadcast([P, NT, D])
                        dve.wait_ge(gates_loaded[s], (it + 1) * 16)
                        reads(d.tensor_tensor(xhat[s][:], ps, gate, ALU.mult), key)
                        brought(dve, it, key)
                        d.tensor_tensor(x[s][:], x[s][:], xhat[s][:], ALU.add).then_inc(x_added[s], 1)
                        return
                    d.tensor_tensor(x[s][:], ps, x[s][:], ALU.add).then_inc(bank_read[BANKS.of[key][0]], 1)
                    brought(dve, it, key)
                    d.nop().then_inc(x_added[s], 1)

                for st in PLAN:
                    if st[0] == "context":
                        context()
                    elif st[0] == "ln":
                        ln(*st[1:])
                    elif st[0] == "qkv":
                        split_q(st[1], st[2], SELF)
                        self_v(st[1], st[2])
                    elif st[0] == "qc":
                        split_q(st[1], st[2], CROSS)
                    elif st[0] == "ctx_k":
                        ctx_k(st[1])
                    elif st[0] == "ctx_v":
                        ctx_v(st[1])
                    elif st[0] == "scores":
                        row_max(*st[1:])
                    elif st[0] == "maxima":
                        maxima(*st[1:])
                    elif st[0] == "norm":
                        norm(*st[1:])
                    elif st[0] == "proj":
                        residual(st[1], st[2], st[3], st)
                    elif st[0] == "down":
                        residual(st[1], st[2], 2, st)

        @block.tensor
        def _(pe):
            t_ = nc.tensor

            def group(out_, pairs):
                for n, (lhsT, rhs) in enumerate(pairs):
                    last = t_.matmul(out_, lhsT, rhs, start=(n == 0), stop=(n == len(pairs) - 1))
                return last

            pe.wait_ge(mod_loads, 16 * len(first))
            pe.wait_ge(pro_dve, 3)
            for n in range(MOD_CHUNKS):
                w = (w_mod if n < 3 else w_ln)[:, :, (n % 3) * 512:(n % 3) * 512 + 512]
                row = 3 if n < 3 else 0
                group(psum[0:B, n, :], [(silu[:, row, k, :], w[:, k, :]) for k in range(KT)]).then_inc(pro_pe, 1)
            pe.wait_ge(w_loads, 16 * len(small + big))
            pe.wait_ge(pro_dve, 4 + MOD_CHUNKS)
            scale_at = (D, 4 * D, 6 * D, 8 * D, 10 * D)
            shift_at = (0, 3 * D, 7 * D, 9 * D, 11 * D)
            for n in range(NORM_SITES):
                for m, at in enumerate((scale_at[n], shift_at[n])):
                    for k in range(KT):
                        col = ((n * 2 + m) * KT + k) * B
                        last = t_.transpose(psum[:, 7, col:col + B], c_rows[:, at + k * P:at + (k + 1) * P], ident[0:B, 0:B])
            last.then_inc(pro_pe, 1)
            pe.wait_ge(mod_all_ready, 1)
            pe.wait_ge(stack_ones, 1)
            pe.wait_ge(identb_ready, 1)
            with pe.Fori(0, ITERS) as it:
                def ln(s, l, i):
                    key = ("ln", s, l, i)
                    pe.wait_ge(xhat_ready[s], it * LAYERS * SITES + site(l, i) + 1)
                    ps = free(pe, it, key)
                    for t in range(NT):
                        for k in range(KT):
                            at = k * N + t * P
                            last = t_.transpose(ps[:, at:at + P], xhat[s][:, t, k * P:(k + 1) * P], ident[:])
                    fills(last, key)

                def project(key, w, at, s):
                    ps = free(pe, it, key)
                    for m in range(KT):
                        last = group(ps[:, m * N:(m + 1) * N], [(w[:, k, at + m * P:at + (m + 1) * P], xT[s][:, k, :]) for k in range(KT)])
                    fills(last, key)

                def qkv(s, l):
                    brought(pe, it, ("ln", s, l, 0))
                    project(("qkv", s, l, "q"), w_qkv[l], 0, s)
                    project(("qkv", s, l, "k"), w_qkv[l], D, s)
                    key = ("qkv", s, l, "v")
                    ps = free(pe, it, key)
                    for t in range(NT):
                        last = group(ps[:, t * D:(t + 1) * D], [(xT[s][:, k, t * P:(t + 1) * P], w_qkv[l][:, k, 2 * D:3 * D]) for k in range(KT)])
                    fills(last, key)

                def ctx_t():
                    pe.wait_ge(ctx_hat_ready, it + 1)
                    ps = free(pe, it, ("ctx_t",))
                    for k in range(KT):
                        for s in per:
                            at = (k * STREAMS + s) * S
                            last = t_.transpose(ps[:, at:at + S], ctx_hat[:, s, k * P:(k + 1) * P], ident[0:S, 0:S])
                    fills(last, ("ctx_t",))

                def ctx_ready(l):
                    if l == 0:
                        brought(pe, it, ("ctx_t",))
                    else:
                        pe.wait_ge(ctxT_loaded, (it + 1) * 16 * STREAMS)

                def ctx_k(l):
                    ctx_ready(l)
                    key = ("ctx_k", l)
                    ps = free(pe, it, key)
                    w = STREAMS * S
                    for m in range(KT):
                        last = group(ps[:, m * w:(m + 1) * w], [(w_kvc[l][:, k, m * P:(m + 1) * P], ctx_T[l][:, k].rearrange("p s n -> p (s n)")) for k in range(KT)])
                    fills(last, key)

                def ctx_v(l):
                    ctx_ready(l)
                    key = ("ctx_v", l)
                    ps = free(pe, it, key)
                    for s in per:
                        last = group(ps[0:S, s * D:(s + 1) * D], [(ctx_T[l][:, k, s, :], w_kvc[l][:, k, D:2 * D]) for k in range(KT)])
                    fills(last, key)

                def q_stacked(s, l, c):
                    sides = len(TERMS)
                    pe.wait_ge(stacked[s], (it * 6 * sides + 3 * sides * l + (2 if c == SELF else 3) * sides) * 16)
                    if c == CROSS:
                        pe.wait_ge(kc_stacked, 16 * AHEAD + (it * LAYERS + l + 1) * 16 * sides * STREAMS)

                def scores(s, l, c, j):
                    key = ("scores", s, l, c, j)
                    if j == 0:
                        q_stacked(s, l, c)
                    ps = free(pe, it, key)
                    for h in ([j] if c == SELF else [2 * j, 2 * j + 1]):
                        for t in range(NT):
                            q = stack[s][0:TROWS, 0, slot(h), t * P:(t + 1) * P]
                            if c == SELF:
                                last = t_.matmul(ps[:, t * N:(t + 1) * N], q, stack[s][0:TROWS, 1, slot(h), :], start=True, stop=True)
                            else:
                                at = (h % 2) * 2 * P + t * P
                                last = t_.matmul(ps[:, at:at + S], q, kc_stack[l][s][0:TROWS, slot(h), :], start=True, stop=True)
                    fills(last, key)

                def maxima(s, l, c):
                    key = ("maxima", s, l, c)
                    pe.wait_ge(nparts_ready[s], it * 4 + event(l, c) + 1)
                    ps = free(pe, it, key)[0:2 * NH, 0:N // 2].bitcast(BF16)
                    for t in range(NT):
                        last = t_.transpose(ps[:, t * P:(t + 1) * P], nparts[s][:, t].rearrange("p a h -> p (a h)"), identb[:])
                    fills(last, key)

                def probs_(s, l, c, g):
                    if g == 0:
                        pe.wait_ge(n_stacked[s], (it * 4 + event(l, c) + 1) * 32)
                    for u in range(QUAD if c == SELF else QUAD // 2):
                        key = ("probs", s, l, c, g, u)
                        ps = free(pe, it, key)
                        if c == SELF:
                            h = head_of(g, u)[0]
                            q = stack[s][0:MROWS, 0, slot(h), :]
                            for t in range(NT):
                                last = t_.matmul(ps[:, t * N:(t + 1) * N], stack[s][0:MROWS, 1, slot(h), t * P:(t + 1) * P], q, start=True, stop=True)
                        else:
                            for w in range(2):
                                h = head_of(g, 2 * u + w)[0]
                                last = t_.matmul(ps[0:S, w * N:(w + 1) * N], kc_stack[l][s][:, slot(h), :], stack[s][0:MROWS, 0, slot(h), :], start=True, stop=True)
                        fills(last, key)

                def pv(s, l, c, g):
                    buf = PROBS.of[(s, l, c, g)][0]
                    if g == 0:
                        free(pe, it, ("out", s, l, c))
                        free(pe, it, ("den", s, l, c))
                        brought(pe, it, ("qkv", s, l, "v") if c == SELF else ("ctx_v", l))
                    brought(pe, it, ("probs", s, l, c, g, (QUAD if c == SELF else QUAD // 2) - 1))
                    keys = NT if c == SELF else 1
                    for kind in range(2):
                        for k in range(keys):
                            for t in range(QUAD):
                                _, half, pair, ab = head_of(g, t)
                                whose = half * 2 + ab
                                if c == SELF:
                                    p = probs[:, buf, t, k * N:(k + 1) * N]
                                    w = v[s][:, k, pair, ab * PAIR:(ab + 1) * PAIR]
                                    one = ones[:, whose, :]
                                else:
                                    p = probs[0:S, buf, t, 0:N]
                                    w = vc[l][s][:, pair, ab * PAIR:(ab + 1) * PAIR]
                                    one = ones[0:S, whose, :]
                                rows = slice(t * PAIR, (t + 1) * PAIR)
                                if kind == 0:
                                    last = t_.matmul(psum[rows, OUTB[0], half * N:(half + 1) * N], w, p, start=(ab == 0 and k == 0),
                                                     stop=(ab == 1 and k == keys - 1), tile_position=(0, t * PAIR), skip_group_check=True)
                                else:
                                    last = t_.matmul(psum[rows, DENB[0], 0:N], one, p, start=(g == 0 and k == 0),
                                                     stop=(whose == 3 and k == keys - 1), tile_position=(0, t * PAIR), skip_group_check=True)
                    last.then_inc(probs_used[buf], 1)

                def tokens_out(key, src, w, tiles, s):
                    ps = free(pe, it, key)
                    for t in range(NT):
                        last = group(ps[:, t * D:(t + 1) * D], [(src[:, k, t * P:(t + 1) * P], w[:, k, :]) for k in range(tiles)])
                    fills(last, key)

                def up(s, l, j):
                    key = ("up", s, l, j)
                    if j == 0:
                        brought(pe, it, ("ln", s, l, 2))
                    project(key, w_up[l], j * KT * P, s)

                for st in PLAN:
                    if st[0] == "ln":
                        ln(*st[1:])
                    elif st[0] == "qkv":
                        qkv(*st[1:])
                    elif st[0] == "qc":
                        brought(pe, it, ("ln", st[1], st[2], 1))
                        project(st, w_qc[st[2]], 0, st[1])
                    elif st[0] == "ctx_t":
                        ctx_t()
                    elif st[0] == "ctx_k":
                        ctx_k(st[1])
                    elif st[0] == "ctx_v":
                        ctx_v(st[1])
                    elif st[0] == "scores":
                        scores(*st[1:])
                    elif st[0] == "maxima":
                        maxima(*st[1:])
                    elif st[0] == "probs":
                        probs_(*st[1:])
                    elif st[0] == "pv":
                        pv(*st[1:])
                    elif st[0] == "proj":
                        _, s, l, c = st
                        brought(pe, it, ("out", s, l, c))
                        tokens_out(st, xT[s], w_proj[l][c], KT, s)
                    elif st[0] == "up":
                        up(*st[1:])
                    elif st[0] == "down":
                        _, s, l = st
                        brought(pe, it, ("up", s, l, FT // 2 - 1))
                        tokens_out(st, hT[s], w_down[l], FT, s)


def constants():
    half = HD // 2
    inv = np.float32(1.0) / np.float32(10000.0) ** (np.arange(half, dtype=np.float32) / np.float32(half))
    ang = np.arange(N, dtype=np.float32)[None, :] * inv.astype(np.float32)[:, None]
    rows = np.arange(P) % HD
    sign = np.where(rows < half, -1.0, 1.0).astype(np.float32)[:, None]
    return {"ident": np.eye(P, dtype=np.float32), "cos": np.cos(ang)[rows % half].astype(np.float32), "sin": (np.sin(ang)[rows % half] * sign).astype(np.float32)}


def kernel(**inputs):
    from concourse import bacc
    from concourse.bass_utils import run_bass_kernel_spmd

    def a(name):
        return np.asarray(inputs[name])

    def by_tile(v, n):
        return np.ascontiguousarray(v.reshape(n, P).T)

    arrays = dict(constants())
    arrays["x"], arrays["ctx"] = a("x"), a("ctx_1024")
    arrays["ctxT"] = np.ascontiguousarray(a("ctx_1024").transpose(0, 2, 1))
    arrays["condT"] = np.ascontiguousarray(a("cond_1024").T)
    for new, old in (("w_mod0", "W_mod"), ("w_qkv0", "W_qkv"), ("w_proj0", "W_proj"), ("w_qc0", "W_qc"), ("w_kvc0", "W_kvc"),
                     ("w_cproj0", "W_cproj"), ("w_up0", "W_mlp1"), ("w_down0", "W_mlp2"), ("b_mod0", "b_mod"), ("b_qkv0", "b_qkv"),
                     ("b_proj0", "b_proj"), ("b_kvc0", "b_kvc"), ("b_cproj0", "b_cproj"), ("b_down0", "b_mlp2")):
        arrays[new] = a("L0_xcond_" + old)
    for new, old in (("w_qkv1", "qkv_w"), ("w_proj1", "sa_out_w"), ("w_qc1", "q_w"), ("w_cproj1", "ca_out_w"), ("w_up1", "ffn_w1"),
                     ("w_down1", "ffn_w2"), ("w_ln0", "ln1_w"), ("w_ln1", "ln2_w"), ("w_ln2", "ln3_w")):
        arrays[new] = np.ascontiguousarray(a("L1_xcond_" + old).T)
    arrays["w_kvc1"] = np.ascontiguousarray(np.concatenate([a("L1_xcond_k_w").T, a("L1_xcond_v_w").T], axis=1))
    for i in range(SITES):
        arrays[f"b_ln{i}"] = a(f"L1_xcond_ln{i + 1}_b")
    arrays["b_down1"] = a("L1_xcond_ffn_b2")
    arrays["b_qk_cols"] = by_tile(a("L0_xcond_b_qkv")[0:2 * D], 2 * KT)
    arrays["b_qc_cols"] = by_tile(a("L0_xcond_b_qc"), KT)
    arrays["b_kc_cols"] = by_tile(a("L0_xcond_b_kvc")[0:D], KT)
    arrays["b_up0_cols"] = by_tile(a("L0_xcond_b_mlp1"), FT)
    arrays["b_up1_cols"] = by_tile(a("L1_xcond_ffn_b1"), FT)

    nc = bacc.Bacc("TRN2", target_bir_lowering=False, num_devices=1)
    ins = {name: nc.dram_tensor("in_" + name, v.shape, mybir.dt.from_np(v.dtype), kind="ExternalInput").ap()
           for name, v in arrays.items()}
    out = nc.dram_tensor("out", (B, N, D), F32, kind="ExternalOutput").ap()
    build(nc, ins, out)
    r = run_bass_kernel_spmd(nc, [{"in_" + name: v for name, v in arrays.items()}], core_ids=[0])
    return r.results[0]["out"]
```

```python
from contextlib import ExitStack

import numpy as np
import concourse.bass as bass
from concourse import mybir

F32 = mybir.dt.float32
BF16 = mybir.dt.bfloat16
ALU = mybir.AluOpType
ACT = mybir.ActivationFunctionType
AX = mybir.AxisListType

P = 128
B, N, D, NH = 8, 256, 256, 16
HD = D // NH
S = 77
F = 1024
KT = D // P
NT = N // P
FT = F // P
STREAMS = 2
ITERS = B // STREAMS
LAYERS = 2
SITES = 3
SCALE = HD ** -0.5
EPS = (1e-6, 1e-5)
HEADS_A_TILE = P // HD
QUAD = 4
PAIR = 2 * HD
QUADS_A_TILE = HEADS_A_TILE // QUAD
NORM_SITES = 5
TERMS = [(0, 0), (0, 1), (1, 0), (1, 1), (0, 2), (2, 0)]
TROWS = HD * len(TERMS)
MROWS = TROWS + 2
SELF, CROSS = 0, 1
AHEAD = 1
SITES_AHEAD = LAYERS * SITES

NORM_COL = {(0, 0): 0, (0, 2): 1, (1, 0): 2, (1, 1): 3, (1, 2): 4}
PRE = {(0, 0): 0, (0, 1): 1, (0, 2): 2, (1, 2): 3}


def site(l, i):
    return l * SITES + i


NS = {'load': (('DMA', 4500),), 'context': (('DMA', 4200), ('DVE', 1700)), 'stats': (('DVE', 1000), ('Pool', 1300)), 'xhat': (('DVE', 350),), 'ln': (('PE', 500), ('ACT', 900)), 'qkv': (('PE', 5300), ('ACT', 900)), 'qc': (('PE', 1750), ('ACT', 900)), 'ctx_t': (('PE', 300), ('ACT', 300)), 'ctx_k': (('PE', 1000), ('ACT', 500), ('DVE', 1500)), 'ctx_v': (('PE', 1700), ('DVE', 700)), ('split', 0, 0): (('DVE', 3600), ('DMA', 6000)), ('split', 0, 1): (('DVE', 2000), ('DMA', 5000)), ('split', 1, 0): (('DVE', 7500), ('DMA', 6000)), ('split', 1, 1): (('DVE', 4200), ('DMA', 5000)), 'scores': (('PE', 250), ('DVE', 620)), 'nmax': (('DVE', 400),), 'maxima': (('PE', 300), ('ACT', 300), ('DMA', 2300)), ('probs', 0): (('PE', 900), ('ACT', 1200)), ('probs', 1): (('PE', 450), ('ACT', 700)), ('pv', 0): (('PE', 2400),), ('pv', 1): (('PE', 500),), 'norm': (('DVE', 2100),), 'proj': (('PE', 1800),), 'add': (('DVE', 900),), 'up': (('PE', 1800), ('ACT', 800)), 'down': (('PE', 6900),), 'store': (('DMA', 2200),)}
LEAD = {'stats': 0, 'nmax': 0, 'scores': 0, 'up': -500, 'down': 0, 'pv': -1000, 'qkv': 0, 'probs': -1000, 'split': 500, 'norm': 0, 'add': 1000, 'ln': 0, 'maxima': 2000}
SKEW = (0, 0)


def plan():
    A, Z = 0, 1

    def scores(s, l, c):
        n = NH if c == SELF else NH // 2
        return [("scores", s, l, c, j) for j in range(n)] + [("nmax", s, l, c), ("maxima", s, l, c)]

    def attend(s, l, c):
        out = [("probs", s, l, c, 0)]
        for g in range(1, NH // QUAD):
            out += [("probs", s, l, c, g), ("pv", s, l, c, g - 1)]
            if g == QUADS_A_TILE + 1:
                out.append(("norm", s, l, c, 0))
        return out + [("pv", s, l, c, NH // QUAD - 1), ("norm", s, l, c, 1), ("proj", s, l, c), ("add", s, l, c)]

    def ln(s, l, i):
        return [("stats", s, l, i), ("xhat", s, l, i), ("ln", s, l, i)]

    begin = [[("load", s)] + ln(s, 0, 0) + [("qkv", s, 0), ("split", s, 0, SELF)] for s in (A, Z)]
    begin[A] = [("load", A), ("context",)] + begin[A][1:] + [("ctx_t",), ("ctx_k", 0), ("ctx_v", 0)]

    def blocks(s):
        out = []
        for l in range(LAYERS):
            if l:
                out += ln(s, l, 0) + [("qkv", s, l), ("split", s, l, SELF)] + scores(s, l, SELF)
            out += attend(s, l, SELF) + ln(s, l, 1) + [("qc", s, l), ("split", s, l, CROSS)]
            if (s, l) == (A, 0):
                out += [("ctx_k", 1), ("ctx_v", 1)]
            out += scores(s, l, CROSS) + attend(s, l, CROSS) + ln(s, l, 2)
            out += [("up", s, l, j) for j in range(FT // 2)] + [("down", s, l), ("add", s, l, 2)]
        return out + [("store", s)]

    def needs(st):
        name = st[0]
        if name == "scores":
            return [("split", *st[1:4])] + ([(*st[:4], st[4] - 2)] if st[4] > 1 else [])
        if name == "probs":
            return [("maxima", *st[1:4])] + ([("pv", *st[1:4], st[4] - 2)] if st[4] > 1 else [])
        if name in ("pv",):
            return [("probs", *st[1:])]
        if name == "norm":
            return [("pv", *st[1:4], (st[4] + 1) * QUADS_A_TILE - 1)]
        if name == "up":
            return [("ln", st[1], st[2], 2)] + ([(*st[:3], st[3] - 2)] if st[3] > 1 else [])
        if name.startswith("ctx"):
            return [("context",), ("ctx_t",)]
        return [None]

    def steps(st):
        return NS.get(st[0]) or (NS[(st[0], *st[2:4])] if st[0] == "split" else NS[st[0], st[3]])

    head = begin[A] + scores(A, 0, SELF)
    lists = [[(st, 0) for st in blocks(A)] + [(st, 1) for st in head],
             [(st, 0) for st in begin[Z] + scores(Z, 0, SELF) + blocks(Z)]]
    at, body, attending = [0, 0], [], None
    busy = dict.fromkeys(("PE", "DVE", "ACT", "Pool"), 0)
    done = [{None: SKEW[s]} for s in (A, Z)]

    def starts(s):
        st = lists[s][at[s]][0]
        ready = max(done[s].get(need, 0) for need in needs(st))
        return max(ready, busy.get(steps(st)[0][0], 0)) - LEAD.get(st[0], 0)

    while at[A] < len(lists[A]) or at[Z] < len(lists[Z]):
        able = [s for s in (A, Z) if at[s] < len(lists[s])
                and not (lists[s][at[s]][0][0] == "probs" and attending not in (None, s))]
        s = min(able, key=starts)
        st, ahead = lists[s][at[s]]
        body.append((st, ahead))
        time = max(done[s].get(need, 0) for need in needs(st))
        for engine, ns in steps(st):
            time = max(time, busy.get(engine, 0)) + ns
            if engine in busy:
                busy[engine] = time
        done[s][st] = time
        if not st[0].startswith("ctx"):
            done[s][None] = time
        at[s] += 1
        if st[0] == "probs":
            attending = s
        elif st[0] == "pv" and st[4] == NH // QUAD - 1:
            attending = None
    return head, body


HEAD, BODY = plan()
ITERATION = HEAD + [st for st, ahead in BODY if not ahead]

OWN, PROB = ((0, 1), (2, 3)), (4, 5)
OUTB = (6, 7)


class Uses:

    def __init__(self):
        self.of, self.per, self.turn = {}, {}, {}

    def give(self, pool, key):
        t = self.turn.get(pool, 0)
        self.turn[pool] = t + 1
        b = pool[t % len(pool)]
        n = self.per.get(b, 0)
        self.per[b] = n + 1
        self.of[key] = (b, n)


def assign():
    banks, probs = Uses(), Uses()
    for st in ITERATION:
        name = st[0]
        own = OWN[0] if name.startswith("ctx") or name == "context" else OWN[st[1]]
        if name in ("ln", "ctx_t", "qc", "proj", "down", "up", "maxima", "ctx_v", "ctx_k", "scores"):
            banks.give(own, st)
        elif name == "qkv":
            for part in "vqk":
                banks.give(own, (*st, part))
        elif name == "probs":
            for u in range(QUAD if st[3] == SELF else QUAD // 2):
                banks.give(PROB, (*st, u))
            probs.give((0, 1), st[1:])
        elif name == "pv" and st[4] % QUADS_A_TILE == 0:
            half = st[4] // QUADS_A_TILE
            banks.give(OUTB[half:half + 1], ("out", *st[1:4], half))
    return banks, probs


BANKS, PROBS = assign()


def head_of(g, t):
    half, ab = g // 2, g % 2
    return half * HEADS_A_TILE + 2 * t + ab, half, half * QUAD + t, ab


def slot(h):
    return (h % HEADS_A_TILE) * KT + h // HEADS_A_TILE


def build(nc, ins, out):
    with ExitStack() as ctx:
        def sb(name, shape, dt=F32):
            return ctx.enter_context(nc.sbuf_tensor(name, shape, dt))

        def sem(name):
            return ctx.enter_context(nc.semaphore(name))

        def both(name):
            return [sem(f"{name}{s}") for s in range(STREAMS)]

        w_qkv = [sb(f"w_qkv{l}", [P, KT, 3 * D]) for l in range(LAYERS)]
        w_proj = [[sb(f"w_proj{l}{c}", [P, KT, D]) for c in range(2)] for l in range(LAYERS)]
        w_qc = [sb(f"w_qc{l}", [P, KT, D]) for l in range(LAYERS)]
        w_kvc = [sb(f"w_kvc{l}", [P, KT, 2 * D]) for l in range(LAYERS)]
        w_up = [sb(f"w_up{l}", [P, KT, F]) for l in range(LAYERS)]
        w_down = [sb(f"w_down{l}", [P, FT, D]) for l in range(LAYERS)]
        ident = sb("ident", [P, P])
        identb = sb("identb", [P, P], BF16)
        cos = sb("cos", [P, N])
        sin = sb("sin", [P, N])
        b_v = sb("b_v", [P, D])
        b_cproj = sb("b_cproj", [P, D])
        b_vc = sb("b_vc", [S, D])
        b_ffn = sb("b_ffn", [P, D])
        b_qk = sb("b_qk", [P, 2 * KT])
        b_qc = sb("b_qc", [P, KT])
        b_kc = sb("b_kc", [P, KT])
        b_up = [sb(f"b_up{l}", [P, FT]) for l in range(LAYERS)]
        ones = sb("ones", [P, 2, PAIR])
        minus_half = sb("minus_half", [P, NT])
        eps_tile = sb("eps_tile", [P, LAYERS, NT])
        spare = sb("spare", [P, 8])
        mod_all = sb("mod_all", [P, NORM_SITES * 2 * KT, B])
        silu = sb("silu", [P, 4, KT, B])
        per = range(STREAMS)
        x = [sb(f"x{s}", [P, NT, D]) for s in per]
        xhat = [sb(f"xhat{s}", [P, NT, D]) for s in per]
        rden = [xhat[s][:].rearrange("p t d -> p (t d)") for s in per]
        xT = [sb(f"xT{s}", [P, KT, N]) for s in per]
        hT = [sb(f"hT{s}", [P, FT, N]) for s in per]
        qk = [hT[s][:, 0:4, :] for s in per]
        rot = [hT[s][:, 4:8, :] for s in per]
        parts = [sb(f"parts{s}", [P, 3, 4, N], BF16) for s in per]
        stack = [sb(f"stack{s}", [P, 2, NH, N], BF16) for s in per]
        v = [sb(f"v{s}", [P, NT, NH // 2, 2 * PAIR]) for s in per]
        gates = [sb(f"gates{s}", [P, 4, D]) for s in per]
        mod = [sb(f"mod{s}", [P, NORM_SITES * 2 * KT]) for s in per]
        kc_stack = [[sb(f"kc_stack{l}{s}", [MROWS, NH, S], BF16) for s in per] for l in range(LAYERS)]
        vc = [[sb(f"vc{l}{s}", [S, NH // 2, 2 * PAIR]) for s in per] for l in range(LAYERS)]
        stats = [sb(f"stats{s}", [P, NT, 6]) for s in per]
        mv = [sb(f"mv{s}", [P, NT, 2]) for s in per]
        rstd = [sb(f"rstd{s}", [P, 2, NT]) for s in per]
        nmax = [sb(f"nmax{s}", [P, NT, NH]) for s in per]
        nparts = [sb(f"nparts{s}", [P, NT, 2, NH], BF16) for s in per]
        nT = [sb(f"nT{s}", [2 * NH, N], BF16) for s in per]
        probs = sb("probs", [P, 2, QUAD, NT * N])
        ctx_in = sb("ctx_in", [S, STREAMS, D])
        ctx_hat = sb("ctx_hat", [S, STREAMS, D])
        ctx_T = [sb(f"ctx_T{l}", [P, KT, STREAMS, S]) for l in range(LAYERS)]
        kc = sb("kc", [P, STREAMS, KT, S])
        kc_rot = sb("kc_rot", [P, STREAMS, KT, S])
        kc_parts = sb("kc_parts", [P, 3, STREAMS, KT, S], BF16)
        c_stats = sb("c_stats", [S, STREAMS, 6])
        c_mv = sb("c_mv", [S, STREAMS, 2])
        c_rstd = sb("c_rstd", [S, 2, STREAMS])
        w_mod = probs[:].rearrange("p a b c -> p (a b c)")[:, 0:KT * 6 * D].rearrange("p (k n) -> p k n", k=KT)
        w_ln = stack[0][:].rearrange("p a b c -> p (a b c)").bitcast(F32)[:, 0:KT * 6 * D].rearrange("p (k n) -> p k n", k=KT)
        c_rows = stack[1][:].rearrange("p a b c -> p (a b c)").bitcast(F32)[0:B, 0:12 * D]
        c_bias = hT[0][:].rearrange("p a b -> p (a b)")[0:B, 0:6 * D]
        c_bias1 = hT[1][:].rearrange("p a b -> p (a b)")[0:B, 0:6 * D]
        g_bias = parts[0][:].rearrange("p a b c -> p (a b c)").bitcast(F32)[0:B, 0:2 * D]
        g_rows = parts[1][:].rearrange("p a b c -> p (a b c)").bitcast(F32)[0:B, 0:4 * D]

        psum = ctx.enter_context(nc.psum_tensor("psum", [P, 8, 512], F32))
        qk_dram = [nc.dram_tensor(f"qk_dram{s}", [P, 3, 4 * N], BF16).ap() for s in per]
        kc_dram = nc.dram_tensor("kc_dram", [P, 3, STREAMS * KT * S], BF16).ap()
        g_dram = nc.dram_tensor("gates_dram", [B, 4 * D], F32).ap()

        bank_full = [sem(f"bank_full{b}") for b in range(8)]
        bank_read = [sem(f"bank_read{b}") for b in range(8)]
        probs_used = [sem(f"probs_used{b}") for b in range(2)]
        x_loaded, gates_loaded, stored = both("x_loaded"), both("gates_loaded"), both("stored")
        x_added, x_biased, mod_ready = both("x_added"), both("x_biased"), both("mod_ready")
        stats_done, mv_ready, var_eps, rstd_ready, xhat_ready = (
            both("stats_done"), both("mv_ready"), both("var_eps"), both("rstd_ready"), both("xhat_ready"))
        rope_rot, rope_cos, rope_sin, rope_done = both("rope_rot"), both("rope_cos"), both("rope_sin"), both("rope_done")
        parts_ready, rest_ready, stacked, rden_ready = both("parts_ready"), both("rest_ready"), both("stacked"), both("rden_ready")
        nmax_done, nhigh_done, nparts_ready, n_stacked = (
            both("nmax_done"), both("nhigh_done"), both("nparts_ready"), both("n_stacked"))
        ctx_loaded, ctxT_loaded = sem("ctx_loaded"), sem("ctxT_loaded")
        c_stats_done, c_mv_ready, c_var_eps, c_rstd_ready, ctx_hat_ready = (
            sem("c_stats_done"), sem("c_mv_ready"), sem("c_var_eps"), sem("c_rstd_ready"), sem("ctx_hat_ready"))
        kc_rotated, kc_cos, kc_sin, kc_roped, kc_parts_ready, kc_rest, kc_stacked = (
            sem("kc_rotated"), sem("kc_cos"), sem("kc_sin"), sem("kc_roped"), sem("kc_parts_ready"),
            sem("kc_rest"), sem("kc_stacked"))
        written = [[sem(f"written{s}{p}") for p in range(3)] for s in per]
        kc_written = [sem(f"kc_written{p}") for p in range(3)]
        mod_loads, w_loads = sem("mod_loads"), sem("w_loads")
        pro_exp, pro_dve, pro_pe, pro_free, pro_gates = (
            sem("pro_exp"), sem("pro_dve"), sem("pro_pe"), sem("pro_free"), sem("pro_gates"))
        identb_ready = sem("identb_ready")
        zeros_ready, consts_ready, mod_all_ready, stack_ones = sem("zeros_ready"), sem("consts_ready"), sem("mod_all_ready"), sem("stack_ones")

        def full(eng, it, key):
            b, n = BANKS.of[key]
            eng.wait_ge(bank_full[b], it * BANKS.per[b] + n + 1)
            return psum[:, b, :]

        def free(eng, it, key):
            b, n = BANKS.of[key]
            eng.wait_ge(bank_read[b], it * BANKS.per[b] + n + AHEAD)
            return psum[:, b, :]

        def fills(ins_, key):
            ins_.then_inc(bank_full[BANKS.of[key][0]], 1)

        def reads(ins_, key):
            ins_.then_inc(bank_read[BANKS.of[key][0]], 1)

        def brought(eng, it, key):
            b, n = BANKS.of[key]
            eng.wait_ge(bank_read[b], it * BANKS.per[b] + n + 1 + AHEAD)

        def carry_wait(n):
            nc.vector.tensor_copy(spare[:, n:n + 1], spare[:, 0:1])

        def event(l, c):
            return l * 2 + c

        def cols(ap):
            return ap.rearrange("(k p) n -> p k n", p=P)

        small = [
            (ident[:], ins["ident"]), (cos[:], ins["cos"]), (sin[:], ins["sin"]),
            (b_v[:], ins["b_qkv0"][2 * D:3 * D].partition_broadcast(P)),
            (b_cproj[:], ins["b_cproj0"][0:D].partition_broadcast(P)),
            (b_vc[:], ins["b_kvc0"][D:2 * D].partition_broadcast(S)),
            (b_ffn[:], ins["b_down1"][0:D].partition_broadcast(P)),
            (b_qk[:], ins["b_qk_cols"]), (b_qc[:], ins["b_qc_cols"]), (b_kc[:], ins["b_kc_cols"]),
            (b_up[0][:], ins["b_up0_cols"]), (b_up[1][:], ins["b_up1_cols"]),
        ]
        big = []
        for l in range(LAYERS):
            big += [(w_qkv[l][:], cols(ins[f"w_qkv{l}"])), (w_kvc[l][:], cols(ins[f"w_kvc{l}"])),
                    (w_qc[l][:], cols(ins[f"w_qc{l}"])), (w_proj[l][0][:], cols(ins[f"w_proj{l}"])),
                    (w_proj[l][1][:], cols(ins[f"w_cproj{l}"])), (w_up[l][:], cols(ins[f"w_up{l}"])),
                    (w_down[l][:], cols(ins[f"w_down{l}"]))]
        first = [(silu[:, 0, :, :], ins["condT"].rearrange("(k p) b -> p k b", p=P)),
                 (w_mod, cols(ins["w_mod0"])), (c_bias, ins["b_mod0"][0:6 * D].partition_broadcast(B)),
                 (g_bias[:, 0:D], ins["b_proj0"][0:D].partition_broadcast(B)),
                 (g_bias[:, D:2 * D], ins["b_down0"][0:D].partition_broadcast(B))]
        for i in range(SITES):
            first.append((w_ln[:, :, i * 2 * D:(i + 1) * 2 * D], cols(ins[f"w_ln{i}"])))
            first.append((c_bias1[:, i * 2 * D:(i + 1) * 2 * D], ins[f"b_ln{i}"][0:2 * D].partition_broadcast(B)))
        MOD_CHUNKS = 6

        block = ctx.enter_context(nc.Block())

        @block.sync
        def _(sp):
            for dst, src in first:
                sp.dma_start(dst, src).then_inc(mod_loads, 16)
            for dst, src in small + big:
                sp.dma_start(dst, src).then_inc(w_loads, 16)
            sp.wait_ge(pro_gates, 1)
            sp.dma_start(g_dram, g_rows).then_inc(pro_free, 16)
            sp.wait_ge(pro_free, 16)
            sp.wait_ge(stack_ones, 1)

            def stage(it, st):
                def load(s):
                    sp.wait_ge(stored[s], (it + AHEAD) * 16)
                    sp.dma_start(x[s][:], ins["x"][it * STREAMS + s].rearrange("(t p) d -> p t d", p=P)).then_inc(x_loaded[s], 16)
                    sp.dma_start(gates[s][:], g_dram[it * STREAMS + s].partition_broadcast(P)).then_inc(gates_loaded[s], 16)

                def context():
                    sp.wait_ge(x_added[0], it * LAYERS * SITES + SITES_AHEAD)
                    for s in per:
                        sp.dma_start(ctx_in[:, s, :], ins["ctx"][it * STREAMS + s]).then_inc(ctx_loaded, 16)
                        sp.dma_start(ctx_T[1][:, :, s, :], ins["ctxT"][it * STREAMS + s].rearrange("(k p) n -> p k n", p=P)).then_inc(ctxT_loaded, 16)

                def through_dram(src, dram, ready, base, written, before, gather):
                    for part in range(3):
                        sp.wait_ge(ready, base + part + 1)
                        sp.dma_start(dram[:, part], src[:, part]).then_inc(written[part], 16)
                    for part in range(3):
                        sp.wait_ge(written[part], (before + 1) * 16)
                        gather(part)

                def by_head(dram, part, at, w):
                    row = dram.ap[0][0]
                    return bass.AP(dram.tensor, dram.offset + part * dram.ap[1][0] + at, [[row, HD], [HD * row, HEADS_A_TILE], [1, w]])

                def stack_q(s, l, c):
                    e = event(l, c)
                    n = 4 if c == SELF else 2

                    def gather(part):
                        for t, term in enumerate(TERMS):
                            for side in range(2 if c == SELF else 1):
                                if term[side] == part:
                                    dst = stack[s][t * HD:(t + 1) * HD, side].rearrange("d (h m) n -> d h (m n)", m=KT)
                                    sp.dma_start(dst, by_head(qk_dram[s], part, side * KT * N, KT * N)).then_inc(stacked[s], 16)

                    through_dram(parts[s][:, :, 0:n, :].rearrange("p a m n -> p a (m n)"), qk_dram[s][:, :, 0:n * N],
                                 parts_ready[s], it * 12 + 3 * e, written[s], it * 4 + e, gather)

                def stack_kc(l):
                    for s in per:
                        sp.wait_ge(x_added[s], it * LAYERS * SITES + site(l, 1) + 1)
                    def gather(part):
                        for t, term in enumerate(TERMS):
                            if term[1] == part:
                                for s in per:
                                    dst = kc_stack[l][s][t * HD:(t + 1) * HD].rearrange("d (h m) n -> d h (m n)", m=KT)
                                    sp.dma_start(dst, by_head(kc_dram, part, s * KT * S, KT * S)).then_inc(kc_stacked, 16)

                    through_dram(kc_parts[:].rearrange("p a s k n -> p a (s k n)"), kc_dram, kc_parts_ready, it * 6 + 3 * l + AHEAD,
                                 kc_written, it * LAYERS + l, gather)

                def stack_maxima(s, l, c):
                    brought(sp, it, ("maxima", s, l, c))
                    for part in range(2):
                        sp.dma_start(stack[s][TROWS + part:TROWS + part + 1, 0, :, :], nT[s][part * NH:(part + 1) * NH, :]).then_inc(n_stacked[s], 16)

                def store(s):
                    sp.wait_ge(x_added[s], (it + 1) * LAYERS * SITES + SITES_AHEAD)
                    sp.dma_start(out[it * STREAMS + s].rearrange("(t p) d -> p t d", p=P), x[s][:]).then_inc(stored[s], 16)

                if st[0] == "load":
                    load(st[1])
                elif st[0] == "context":
                    context()
                elif st[0] == "split":
                    stack_q(*st[1:])
                elif st[0] == "ctx_k":
                    stack_kc(st[1])
                elif st[0] == "maxima":
                    stack_maxima(*st[1:])
                elif st[0] == "store":
                    store(st[1])

            for st in HEAD:
                stage(0, st)
            with sp.Fori(0, ITERS - 1) as it:
                for st, ahead in BODY:
                    stage(it + 1 if ahead else it, st)
            for st, ahead in BODY:
                if not ahead:
                    stage(ITERS - 1, st)
            for s in per:
                sp.wait_ge(stored[s], (ITERS + AHEAD) * 16)

        @block.gpsimd
        def _(pool):
            g = nc.gpsimd
            pool.wait_ge(w_loads, 16 * len(small + big))
            pool.wait_ge(consts_ready, 1)
            pool.wait_ge(mod_all_ready, 1)
            def stage(it, st):
                def load(s):
                    pool.wait_ge(x_added[s], it * LAYERS * SITES + SITES_AHEAD)
                    g.tensor_copy(mod[s][:], mod_all[:, :, it * STREAMS + s]).then_inc(mod_ready[s], 1)

                def inv_std(mv_, r, ready, eps_done, done, e, per_it, eps, n):
                    pool.wait_ge(ready, it * per_it + e + 1)
                    g.tensor_tensor(r[:, 0, :], mv_[:, :, 1], eps, ALU.add).then_inc(eps_done, 1)
                    pool.wait_ge(eps_done, it * per_it + e + 1)
                    g.tensor_tensor(r[:, 1, :], r[:, 0, :], minus_half[0:n, :], ALU.pow).then_inc(done, 1)

                def ln_std(s, l, i):
                    inv_std(mv[s], rstd[s], mv_ready[s], var_eps[s], rstd_ready[s], site(l, i), LAYERS * SITES, eps_tile[:, l, :], P)

                def add_bias(s, l, i):
                    if (l, i) in PRE:
                        pool.wait_ge(xhat_ready[s], it * LAYERS * SITES + site(l, i) + 1)
                        if (l, i) == (0, 0):
                            pool.wait_ge(gates_loaded[s], (it + 1) * 16)
                        bias = {(0, 0): gates[s][:, 1, :], (0, 1): b_cproj[:], (0, 2): gates[s][:, 3, :], (1, 2): b_ffn[:]}[(l, i)]
                        for t in range(NT):
                            last = g.tensor_tensor(x[s][:, t, :], x[s][:, t, :], bias, ALU.add)
                        last.then_inc(x_biased[s], 1)

                def rope(s, l, c):
                    if l == 1:
                        n = 4 if c == SELF else 2
                        pool.wait_ge(rope_rot[s], it * 2 + c + 1)
                        for m in range(n):
                            last = g.tensor_tensor(qk[s][:, m, :], qk[s][:, m, :], cos[:], ALU.mult)
                        last.then_inc(rope_cos[s], 1)

                if st[0] == "load":
                    load(st[1])
                elif st[0] == "context":
                    inv_std(c_mv, c_rstd, c_mv_ready, c_var_eps, c_rstd_ready, 0, 1, eps_tile[0:S, 0, :], S)
                elif st[0] == "stats":
                    ln_std(*st[1:])
                elif st[0] == "xhat":
                    add_bias(*st[1:])
                elif st[0] == "split":
                    rope(*st[1:])

            for st in HEAD:
                stage(0, st)
            with pool.Fori(0, ITERS - 1) as it:
                for st, ahead in BODY:
                    stage(it + 1 if ahead else it, st)
            for st, ahead in BODY:
                if not ahead:
                    stage(ITERS - 1, st)

        @block.scalar
        def _(act):
            a = nc.scalar
            act.wait_ge(mod_loads, 16 * len(first))
            a.activation(silu[:, 1], silu[:, 0], ACT.Exp, scale=-1.0).then_inc(pro_exp, 1)
            act.wait_ge(w_loads, 16 * len(small + big))
            def stage(it, st):
                def ln(s, l, i):
                    ps = full(act, it, ("ln", s, l, i))
                    if (l, i) == (0, 0):
                        act.wait_ge(mod_ready[s], it + 1)
                    if (l, i) in NORM_COL:
                        col = NORM_COL[(l, i)] * 2 * KT
                        for k in range(KT):
                            last = a.activation(xT[s][:, k, :], ps[:, k * N:(k + 1) * N], ACT.Identity,
                                                scale=mod[s][:, col + k:col + k + 1],
                                                bias=mod[s][:, col + KT + k:col + KT + k + 1])
                    else:
                        last = a.activation(xT[s][:].rearrange("p k n -> p (k n)"), ps, ACT.Copy)
                    reads(last, ("ln", s, l, i))

                def q_out(s, l, c):
                    for part in ("q", "k") if c == SELF else ("q",):
                        key = ("qkv", s, l, part) if c == SELF else ("qc", s, l)
                        ps = full(act, it, key)
                        m0 = 0 if part == "q" else KT
                        if l == 0:
                            bias = b_qk if c == SELF else b_qc
                            for m in range(KT):
                                last = a.activation(qk[s][:, m0 + m, :], ps[:, m * N:(m + 1) * N], ACT.Identity,
                                                    bias=bias[:, m0 + m:m0 + m + 1])
                        else:
                            last = a.activation(qk[s][:, m0:m0 + KT, :].rearrange("p m n -> p (m n)"), ps, ACT.Copy)
                        reads(last, key)

                def ctx_t():
                    ps = full(act, it, ("ctx_t",))
                    reads(a.activation(ctx_T[0][:].rearrange("p k s n -> p (k s n)"), ps[:, 0:KT * STREAMS * S], ACT.Copy), ("ctx_t",))

                def kc_out(l):
                    ps = full(act, it, ("ctx_k", l))
                    act.wait_ge(kc_parts_ready, it * 6 + l * 3 + AHEAD)
                    for m in range(KT):
                        src = ps[:, m * STREAMS * S:(m + 1) * STREAMS * S].rearrange("p (s n) -> p s n", s=STREAMS)
                        if l == 0:
                            last = a.activation(kc[:, :, m, :], src, ACT.Identity, bias=b_kc[:, m:m + 1])
                        else:
                            last = a.activation(kc[:, :, m, :], src, ACT.Copy)
                    reads(last, ("ctx_k", l))

                def maxima(s, l, c):
                    ps = full(act, it, ("maxima", s, l, c))
                    src = ps[0:2 * NH, 0:N // 2].bitcast(BF16)
                    reads(a.activation(nT[s][:], src, ACT.Copy), ("maxima", s, l, c))

                def exps(s, l, c, g):
                    buf, n = PROBS.of[(s, l, c, g)]
                    act.wait_ge(probs_used[buf], it * PROBS.per[buf] + n + AHEAD)
                    for u in range(QUAD if c == SELF else QUAD // 2):
                        key = ("probs", s, l, c, g, u)
                        ps = full(act, it, key)
                        if c == SELF:
                            last = a.activation(probs[:, buf, u, :], ps, ACT.Exp, scale=SCALE)
                        else:
                            last = a.activation(probs[0:S, buf, 2 * u:2 * u + 2, 0:N],
                                                ps[0:S, :].rearrange("p (h n) -> p h n", h=2), ACT.Exp, scale=SCALE)
                        reads(last, key)

                def gelu(s, l, j):
                    ps = full(act, it, ("up", s, l, j))
                    fn = ACT.Gelu_apprx_tanh if l == 0 else ACT.Gelu
                    for m in range(2):
                        f = 2 * j + m
                        last = a.activation(hT[s][:, f, :], ps[:, m * N:(m + 1) * N], fn, bias=b_up[l][:, f:f + 1])
                    reads(last, ("up", s, l, j))

                if st[0] == "ln":
                    ln(*st[1:])
                elif st[0] == "qkv":
                    q_out(st[1], st[2], SELF)
                elif st[0] == "qc":
                    q_out(st[1], st[2], CROSS)
                elif st[0] == "ctx_t":
                    ctx_t()
                elif st[0] == "ctx_k":
                    kc_out(st[1])
                elif st[0] == "maxima":
                    maxima(*st[1:])
                elif st[0] == "probs":
                    exps(*st[1:])
                elif st[0] == "up":
                    gelu(*st[1:])

            for st in HEAD:
                stage(0, st)
            with act.Fori(0, ITERS - 1) as it:
                for st, ahead in BODY:
                    stage(it + 1 if ahead else it, st)
            for st, ahead in BODY:
                if not ahead:
                    stage(ITERS - 1, st)

        @block.vector
        def _(dve):
            d = nc.vector
            d.memset(ones[:], 0.0).then_inc(zeros_ready, 1)
            d.memset(minus_half[:], -0.5)
            d.memset(spare[:], 0.0)
            for l in range(LAYERS):
                d.memset(eps_tile[:, l], EPS[l])
            for s in per:
                d.memset(v[s][:], 0.0)
                for l in range(LAYERS):
                    d.memset(vc[l][s][:], 0.0)
                    d.memset(kc_stack[l][s][TROWS:MROWS], 1.0)
            for sem_ in bank_read + probs_used + [kc_parts_ready]:
                dve.sem_inc(sem_, AHEAD)
            for sem_ in x_added:
                dve.sem_inc(sem_, SITES_AHEAD)
            for sem_ in stored + [kc_stacked]:
                dve.sem_inc(sem_, 16 * AHEAD)
            dve.wait_ge(zeros_ready, 1)
            for n in range(2):
                last = d.memset(ones[:, n, n * HD:(n + 1) * HD], 1.0)
            last.then_inc(consts_ready, 1)
            dve.wait_ge(pro_exp, 1)
            d.tensor_scalar(silu[:, 2], silu[:, 1], 1.0, None, ALU.add).then_inc(pro_dve, 1)
            dve.wait_ge(pro_dve, 1)
            d.reciprocal(silu[:, 1], silu[:, 2]).then_inc(pro_dve, 1)
            dve.wait_ge(pro_dve, 2)
            d.tensor_tensor(silu[:, 3], silu[:, 0], silu[:, 1], ALU.mult).then_inc(pro_dve, 1)
            bias_rows = [c_bias, c_bias1]
            for n in range(MOD_CHUNKS):
                dve.wait_ge(pro_pe, n + 1)
                bias = bias_rows[n // 3][:, (n % 3) * 512:(n % 3) * 512 + 512]
                d.tensor_tensor(c_rows[:, n * 512:(n + 1) * 512], psum[0:B, n, :], bias, ALU.add).then_inc(pro_dve, 1)
            dve.wait_ge(pro_dve, 3 + MOD_CHUNKS)
            gate_at = (2 * D, 5 * D)
            scale_at = (D, 4 * D, 6 * D, 8 * D, 10 * D)
            shift_at = (0, 3 * D, 7 * D, 9 * D, 11 * D)
            for at in scale_at:
                last = d.tensor_scalar(c_rows[:, at:at + D], c_rows[:, at:at + D], 1.0, None, ALU.add)
            last.then_inc(pro_dve, 1)
            for n, at in enumerate(gate_at):
                d.tensor_copy(g_rows[:, 2 * n * D:(2 * n + 1) * D], c_rows[:, at:at + D])
                last = d.tensor_tensor(g_rows[:, (2 * n + 1) * D:(2 * n + 2) * D], c_rows[:, at:at + D], g_bias[:, n * D:(n + 1) * D], ALU.mult)
            last.then_inc(pro_gates, 1)
            dve.wait_ge(pro_pe, MOD_CHUNKS + 1)
            d.tensor_copy(mod_all[:], psum[:, 7, 0:NORM_SITES * 2 * KT * B].rearrange("p (c b) -> p c b", b=B)).then_inc(mod_all_ready, 1)
            dve.wait_ge(pro_gates, 1)
            for s in per:
                last = d.memset(stack[s][TROWS:MROWS, 1], 1.0)
            last.then_inc(stack_ones, 1)
            dve.wait_ge(w_loads, 16 * len(small + big))
            d.tensor_copy(identb[:], ident[:]).then_inc(identb_ready, 1)
            dve.wait_ge(consts_ready, 1)
            def stage(it, st):
                def moments(src, st_, mv_, sems, e, per_it, who):
                    done, mvr = sems
                    for t in range(2):
                        last = d.bn_stats(st_[:, t, :], src[:, t, :])
                    last.then_inc(done, 1)
                    dve.wait_ge(done, it * per_it + e + 1)
                    carry_wait(who)
                    for t in range(2):
                        last = d.bn_aggr(mv_[:, t, :], st_[:, t, :])
                    last.then_inc(mvr, 1)

                def normalise(src, mv_, r, dst, sems, e, per_it):
                    mvr, eps_ready, ready = sems
                    dve.wait_ge(mvr, it * per_it + e + 1)
                    dve.wait_ge(eps_ready, it * per_it + e + 1)
                    for t in range(2):
                        last = d.tensor_scalar(dst[:, t, :], src[:, t, :], mv_[:, t, 0:1], r[:, 1, t:t + 1], ALU.subtract, ALU.mult)
                    last.then_inc(ready, 1)

                def ln_stats(s, l, i):
                    e = site(l, i)
                    if e == 0:
                        dve.wait_ge(x_loaded[s], (it + 1) * 16)
                    else:
                        dve.wait_ge(x_added[s], it * LAYERS * SITES + e + SITES_AHEAD)
                    moments(x[s], stats[s], mv[s], (stats_done[s], mv_ready[s]), e, LAYERS * SITES, 1 + s)

                def ln_xhat(s, l, i):
                    normalise(x[s], mv[s], rstd[s], xhat[s], (mv_ready[s], rstd_ready[s], xhat_ready[s]), site(l, i), LAYERS * SITES)

                def context():
                    dve.wait_ge(ctx_loaded, (it + 1) * 16 * STREAMS)
                    moments(ctx_in, c_stats, c_mv, (c_stats_done, c_mv_ready), 0, 1, 3)
                    normalise(ctx_in, c_mv, c_rstd, ctx_hat, (c_mv_ready, c_rstd_ready, ctx_hat_ready), 0, 1)

                def split(src, n, dst, rest_sem, ready, base_rest, base_ready):
                    d.tensor_copy(dst[0], src).then_inc(ready, 1)
                    dve.wait_ge(ready, base_ready + 1)
                    d.tensor_tensor(src, src, dst[0], ALU.subtract).then_inc(rest_sem, 1)
                    dve.wait_ge(rest_sem, base_rest + 1)
                    d.tensor_copy(dst[1], src).then_inc(ready, 1)
                    dve.wait_ge(ready, base_ready + 2)
                    d.tensor_tensor(dst[2], src, dst[1], ALU.subtract).then_inc(ready, 1)

                SWAP = [i ^ (HD // 2) for i in range(32)]

                def split_q(s, l, c):
                    n = 4 if c == SELF else 2
                    brought(dve, it, ("qkv", s, l, "k") if c == SELF else ("qc", s, l))
                    if l == 1:
                        carry_wait(4 + s)
                    src = qk[s][:, 0:n, :]
                    if l == 1:
                        e = it * 2 + c + 1
                        turned = rot[s][:, 0:n, :]
                        d.stream_shuffle(turned, src, SWAP).then_inc(rope_rot[s], 1)
                        dve.wait_ge(rope_rot[s], e)
                        d.tensor_tensor(turned, turned, sin[:].unsqueeze(1).to_broadcast([P, n, N]), ALU.mult).then_inc(rope_sin[s], 1)
                        dve.wait_ge(rope_sin[s], e)
                        dve.wait_ge(rope_cos[s], e)
                        d.tensor_tensor(src, src, turned, ALU.add).then_inc(rope_done[s], 1)
                        dve.wait_ge(rope_done[s], e)
                    ev = event(l, c)
                    split(src, n, [parts[s][:, p, 0:n, :] for p in range(3)], rest_ready[s], parts_ready[s],
                          it * 4 + ev, it * 12 + 3 * ev)

                def v_out(ps, dst, bias, n):
                    to = bass.AP(dst.tensor, dst.offset, [dst.ap[0], [2 * PAIR, NH // 2], [PAIR + HD, 2], [1, HD]])
                    frm = ps.rearrange("p (h a d) -> p h a d", a=2, d=HD)
                    if bias is None:
                        return d.tensor_copy(to, frm)
                    return d.tensor_tensor(to, frm, bias.rearrange("p (h a d) -> p h a d", a=2, d=HD), ALU.add)

                def self_v(s, l):
                    key = ("qkv", s, l, "v")
                    ps = full(dve, it, key)
                    for t in range(NT):
                        last = v_out(ps[:, t * D:(t + 1) * D], v[s][:, t], b_v[:] if l == 0 else None, P)
                    reads(last, key)

                def ctx_v(l):
                    key = ("ctx_v", l)
                    for s in per:
                        dve.wait_ge(x_added[s], it * LAYERS * SITES + site(l, 1) + 1)
                    ps = full(dve, it, key)
                    for s in per:
                        last = v_out(ps[0:S, s * D:(s + 1) * D], vc[l][s][:], b_vc[:] if l == 0 else None, S)
                    reads(last, key)

                def ctx_k(l):
                    brought(dve, it, ("ctx_k", l))
                    if l == 1:
                        carry_wait(6)
                    src = kc[:].rearrange("p s k n -> p (s k) n")
                    if l == 1:
                        turned = kc_rot[:].rearrange("p s k n -> p (s k) n")
                        wide = [P, STREAMS * KT, S]
                        d.stream_shuffle(turned, src, SWAP).then_inc(kc_rotated, 1)
                        dve.wait_ge(kc_rotated, it + 1)
                        d.tensor_tensor(turned, turned, sin[:, 0:S].unsqueeze(1).to_broadcast(wide), ALU.mult).then_inc(kc_sin, 1)
                        d.tensor_tensor(src, src, cos[:, 0:S].unsqueeze(1).to_broadcast(wide), ALU.mult).then_inc(kc_cos, 1)
                        dve.wait_ge(kc_sin, it + 1)
                        dve.wait_ge(kc_cos, it + 1)
                        d.tensor_tensor(src, src, turned, ALU.add).then_inc(kc_roped, 1)
                        dve.wait_ge(kc_roped, it + 1)
                    dve.wait_ge(kc_stacked, 16 * AHEAD + (it * LAYERS + l) * 16 * len(TERMS) * STREAMS)
                    split(src, None, [kc_parts[:, p].rearrange("p s k n -> p (s k) n") for p in range(3)], kc_rest, kc_parts_ready,
                          it * LAYERS + l, it * 6 + 3 * l + AHEAD)

                def row_max(s, l, c, j):
                    key = ("scores", s, l, c, j)
                    ps = full(dve, it, key)
                    if c == SELF:
                        last = d.tensor_reduce(nmax[s][:, :, slot(j)], ps.rearrange("p (t n) -> p t n", t=NT), AX.X, ALU.max, negate=True)
                    else:
                        for h in range(2):
                            src = ps[:, h * 2 * P:(h + 1) * 2 * P].rearrange("p (t n) -> p t n", t=NT)[:, :, 0:S]
                            last = d.tensor_reduce(nmax[s][:, :, slot(2 * j + h)], src, AX.X, ALU.max, negate=True)
                    reads(last, key)

                def maxima(s, l, c):
                    e = it * 4 + event(l, c) + 1
                    last_j = (NH if c == SELF else NH // 2) - 1
                    brought(dve, it, ("scores", s, l, c, last_j))
                    d.tensor_copy(nparts[s][:, :, 0, :], nmax[s][:]).then_inc(nhigh_done[s], 1)
                    dve.wait_ge(nhigh_done[s], e)
                    d.tensor_tensor(nparts[s][:, :, 1, :], nmax[s][:], nparts[s][:, :, 0, :], ALU.subtract).then_inc(nparts_ready[s], 1)

                def norm(s, l, c, half):
                    key = ("out", s, l, c, half)
                    buf, n = PROBS.of[(s, l, c, (half + 1) * QUADS_A_TILE - 1)]
                    dve.wait_ge(probs_used[buf], it * PROBS.per[buf] + n + 1 + AHEAD)
                    ps = psum[:, OUTB[half], :]
                    inv = rden[s][:, half * N:(half + 1) * N]
                    d.reciprocal(inv, ps[:, N:2 * N]).then_inc(rden_ready[s], 1)
                    dve.wait_ge(rden_ready[s], it * 4 * KT + event(l, c) * KT + half + 1)
                    reads(d.tensor_tensor(xT[s][:, half, :], ps[:, 0:N], inv, ALU.mult), key)

                def residual(s, l, i, key):
                    ps = full(dve, it, key).rearrange("p (t n) -> p t n", t=NT)
                    if (l, i) in PRE:
                        dve.wait_ge(x_biased[s], it * len(PRE) + PRE[(l, i)] + 1)
                    if l == 0 and i != 1:
                        gate = gates[s][:, 0 if i == 0 else 2, :].unsqueeze(1).to_broadcast([P, NT, D])
                        dve.wait_ge(gates_loaded[s], (it + 1) * 16)
                        reads(d.tensor_tensor(xhat[s][:], ps, gate, ALU.mult), key)
                        brought(dve, it, key)
                        d.tensor_tensor(x[s][:], x[s][:], xhat[s][:], ALU.add).then_inc(x_added[s], 1)
                        return
                    d.tensor_tensor(x[s][:], ps, x[s][:], ALU.add).then_inc(bank_read[BANKS.of[key][0]], 1)
                    brought(dve, it, key)
                    d.nop().then_inc(x_added[s], 1)

                if st[0] == "context":
                    context()
                elif st[0] == "stats":
                    ln_stats(*st[1:])
                elif st[0] == "xhat":
                    ln_xhat(*st[1:])
                elif st[0] == "qkv":
                    self_v(st[1], st[2])
                elif st[0] == "split":
                    split_q(*st[1:])
                elif st[0] == "ctx_k":
                    ctx_k(st[1])
                elif st[0] == "ctx_v":
                    ctx_v(st[1])
                elif st[0] == "scores":
                    row_max(*st[1:])
                elif st[0] == "nmax":
                    maxima(*st[1:])
                elif st[0] == "norm":
                    norm(*st[1:])
                elif st[0] == "add":
                    _, s, l, i = st
                    residual(s, l, i, ("down", s, l) if i == 2 else ("proj", s, l, i))

            for st in HEAD:
                stage(0, st)
            with dve.Fori(0, ITERS - 1) as it:
                for st, ahead in BODY:
                    stage(it + 1 if ahead else it, st)
            for st, ahead in BODY:
                if not ahead:
                    stage(ITERS - 1, st)

        @block.tensor
        def _(pe):
            t_ = nc.tensor

            def group(out_, pairs):
                for n, (lhsT, rhs) in enumerate(pairs):
                    last = t_.matmul(out_, lhsT, rhs, start=(n == 0), stop=(n == len(pairs) - 1))
                return last

            pe.wait_ge(mod_loads, 16 * len(first))
            pe.wait_ge(pro_dve, 3)
            for n in range(MOD_CHUNKS):
                w = (w_mod if n < 3 else w_ln)[:, :, (n % 3) * 512:(n % 3) * 512 + 512]
                row = 3 if n < 3 else 0
                group(psum[0:B, n, :], [(silu[:, row, k, :], w[:, k, :]) for k in range(KT)]).then_inc(pro_pe, 1)
            pe.wait_ge(w_loads, 16 * len(small + big))
            pe.wait_ge(pro_dve, 4 + MOD_CHUNKS)
            scale_at = (D, 4 * D, 6 * D, 8 * D, 10 * D)
            shift_at = (0, 3 * D, 7 * D, 9 * D, 11 * D)
            for n in range(NORM_SITES):
                for m, at in enumerate((scale_at[n], shift_at[n])):
                    for k in range(KT):
                        col = ((n * 2 + m) * KT + k) * B
                        last = t_.transpose(psum[:, 7, col:col + B], c_rows[:, at + k * P:at + (k + 1) * P], ident[0:B, 0:B])
            last.then_inc(pro_pe, 1)
            pe.wait_ge(mod_all_ready, 1)
            pe.wait_ge(stack_ones, 1)
            pe.wait_ge(identb_ready, 1)
            def stage(it, st):
                def ln(s, l, i):
                    key = ("ln", s, l, i)
                    pe.wait_ge(xhat_ready[s], it * LAYERS * SITES + site(l, i) + 1)
                    ps = free(pe, it, key)
                    for t in range(NT):
                        for k in range(KT):
                            at = k * N + t * P
                            last = t_.transpose(ps[:, at:at + P], xhat[s][:, t, k * P:(k + 1) * P], ident[:])
                    fills(last, key)

                def project(key, w, at, s):
                    ps = free(pe, it, key)
                    for m in range(KT):
                        last = group(ps[:, m * N:(m + 1) * N], [(w[:, k, at + m * P:at + (m + 1) * P], xT[s][:, k, :]) for k in range(KT)])
                    fills(last, key)

                def qkv(s, l):
                    brought(pe, it, ("ln", s, l, 0))
                    key = ("qkv", s, l, "v")
                    ps = free(pe, it, key)
                    for t in range(NT):
                        last = group(ps[:, t * D:(t + 1) * D], [(xT[s][:, k, t * P:(t + 1) * P], w_qkv[l][:, k, 2 * D:3 * D]) for k in range(KT)])
                    fills(last, key)
                    project(("qkv", s, l, "q"), w_qkv[l], 0, s)
                    project(("qkv", s, l, "k"), w_qkv[l], D, s)

                def ctx_t():
                    pe.wait_ge(ctx_hat_ready, it + 1)
                    ps = free(pe, it, ("ctx_t",))
                    for k in range(KT):
                        for s in per:
                            at = (k * STREAMS + s) * S
                            last = t_.transpose(ps[:, at:at + S], ctx_hat[:, s, k * P:(k + 1) * P], ident[0:S, 0:S])
                    fills(last, ("ctx_t",))

                def ctx_ready(l):
                    if l == 0:
                        brought(pe, it, ("ctx_t",))
                    else:
                        pe.wait_ge(ctxT_loaded, (it + 1) * 16 * STREAMS)

                def ctx_k(l):
                    ctx_ready(l)
                    key = ("ctx_k", l)
                    ps = free(pe, it, key)
                    w = STREAMS * S
                    for m in range(KT):
                        last = group(ps[:, m * w:(m + 1) * w], [(w_kvc[l][:, k, m * P:(m + 1) * P], ctx_T[l][:, k].rearrange("p s n -> p (s n)")) for k in range(KT)])
                    fills(last, key)

                def ctx_v(l):
                    ctx_ready(l)
                    key = ("ctx_v", l)
                    ps = free(pe, it, key)
                    for s in per:
                        last = group(ps[0:S, s * D:(s + 1) * D], [(ctx_T[l][:, k, s, :], w_kvc[l][:, k, D:2 * D]) for k in range(KT)])
                    fills(last, key)

                def q_stacked(s, l, c):
                    sides = len(TERMS)
                    pe.wait_ge(stacked[s], (it * 6 * sides + 3 * sides * l + (2 if c == SELF else 3) * sides) * 16)
                    if c == CROSS:
                        pe.wait_ge(kc_stacked, 16 * AHEAD + (it * LAYERS + l + 1) * 16 * sides * STREAMS)

                def scores(s, l, c, j):
                    key = ("scores", s, l, c, j)
                    if j == 0:
                        q_stacked(s, l, c)
                    ps = free(pe, it, key)
                    for h in ([j] if c == SELF else [2 * j, 2 * j + 1]):
                        for t in range(NT):
                            q = stack[s][0:TROWS, 0, slot(h), t * P:(t + 1) * P]
                            if c == SELF:
                                last = t_.matmul(ps[:, t * N:(t + 1) * N], q, stack[s][0:TROWS, 1, slot(h), :], start=True, stop=True)
                            else:
                                at = (h % 2) * 2 * P + t * P
                                last = t_.matmul(ps[:, at:at + S], q, kc_stack[l][s][0:TROWS, slot(h), :], start=True, stop=True)
                    fills(last, key)

                def maxima(s, l, c):
                    key = ("maxima", s, l, c)
                    pe.wait_ge(nparts_ready[s], it * 4 + event(l, c) + 1)
                    ps = free(pe, it, key)[0:2 * NH, 0:N // 2].bitcast(BF16)
                    for t in range(NT):
                        last = t_.transpose(ps[:, t * P:(t + 1) * P], nparts[s][:, t].rearrange("p a h -> p (a h)"), identb[:])
                    fills(last, key)

                def probs_(s, l, c, g):
                    if g == 0:
                        pe.wait_ge(n_stacked[s], (it * 4 + event(l, c) + 1) * 32)
                    for u in range(QUAD if c == SELF else QUAD // 2):
                        key = ("probs", s, l, c, g, u)
                        ps = free(pe, it, key)
                        if c == SELF:
                            h = head_of(g, u)[0]
                            q = stack[s][0:MROWS, 0, slot(h), :]
                            for t in range(NT):
                                last = t_.matmul(ps[:, t * N:(t + 1) * N], stack[s][0:MROWS, 1, slot(h), t * P:(t + 1) * P], q, start=True, stop=True)
                        else:
                            for w in range(2):
                                h = head_of(g, 2 * u + w)[0]
                                last = t_.matmul(ps[0:S, w * N:(w + 1) * N], kc_stack[l][s][:, slot(h), :], stack[s][0:MROWS, 0, slot(h), :], start=True, stop=True)
                        fills(last, key)

                def pv(s, l, c, g):
                    buf = PROBS.of[(s, l, c, g)][0]
                    half = g // QUADS_A_TILE
                    if g % QUADS_A_TILE == 0:
                        free(pe, it, ("out", s, l, c, half))
                    if g == 0:
                        brought(pe, it, ("qkv", s, l, "v") if c == SELF else ("ctx_v", l))
                    brought(pe, it, ("probs", s, l, c, g, (QUAD if c == SELF else QUAD // 2) - 1))
                    keys = NT if c == SELF else 1
                    for kind in range(2):
                        for k in range(keys):
                            for t in range(QUAD):
                                _, _, pair, ab = head_of(g, t)
                                if c == SELF:
                                    p = probs[:, buf, t, k * N:(k + 1) * N]
                                    w = v[s][:, k, pair, ab * PAIR:(ab + 1) * PAIR]
                                    one = ones[:, ab, :]
                                else:
                                    p = probs[0:S, buf, t, 0:N]
                                    w = vc[l][s][:, pair, ab * PAIR:(ab + 1) * PAIR]
                                    one = ones[0:S, ab, :]
                                rows = slice(t * PAIR, (t + 1) * PAIR)
                                last = t_.matmul(psum[rows, OUTB[half], kind * N:(kind + 1) * N], w if kind == 0 else one, p,
                                                 start=(kind == 0 and ab == 0 and k == 0), stop=(ab == 1 and k == keys - 1),
                                                 tile_position=(0, t * PAIR), skip_group_check=True)
                    last.then_inc(probs_used[buf], 1)

                def tokens_out(key, src, w, tiles, s):
                    ps = free(pe, it, key)
                    for t in range(NT):
                        last = group(ps[:, t * D:(t + 1) * D], [(src[:, k, t * P:(t + 1) * P], w[:, k, :]) for k in range(tiles)])
                    fills(last, key)

                def up(s, l, j):
                    key = ("up", s, l, j)
                    if j == 0:
                        brought(pe, it, ("ln", s, l, 2))
                    project(key, w_up[l], j * KT * P, s)

                if st[0] == "ln":
                    ln(*st[1:])
                elif st[0] == "qkv":
                    qkv(*st[1:])
                elif st[0] == "qc":
                    brought(pe, it, ("ln", st[1], st[2], 1))
                    project(st, w_qc[st[2]], 0, st[1])
                elif st[0] == "ctx_t":
                    ctx_t()
                elif st[0] == "ctx_k":
                    ctx_k(st[1])
                elif st[0] == "ctx_v":
                    ctx_v(st[1])
                elif st[0] == "scores":
                    scores(*st[1:])
                elif st[0] == "maxima":
                    maxima(*st[1:])
                elif st[0] == "probs":
                    probs_(*st[1:])
                elif st[0] == "pv":
                    pv(*st[1:])
                elif st[0] == "proj":
                    _, s, l, c = st
                    for half in range(KT):
                        brought(pe, it, ("out", s, l, c, half))
                    tokens_out(st, xT[s], w_proj[l][c], KT, s)
                elif st[0] == "up":
                    up(*st[1:])
                elif st[0] == "down":
                    _, s, l = st
                    brought(pe, it, ("up", s, l, FT // 2 - 1))
                    tokens_out(st, hT[s], w_down[l], FT, s)

            for st in HEAD:
                stage(0, st)
            with pe.Fori(0, ITERS - 1) as it:
                for st, ahead in BODY:
                    stage(it + 1 if ahead else it, st)
            for st, ahead in BODY:
                if not ahead:
                    stage(ITERS - 1, st)


def constants():
    half = HD // 2
    inv = np.float32(1.0) / np.float32(10000.0) ** (np.arange(half, dtype=np.float32) / np.float32(half))
    ang = np.arange(N, dtype=np.float32)[None, :] * inv.astype(np.float32)[:, None]
    rows = np.arange(P) % HD
    sign = np.where(rows < half, -1.0, 1.0).astype(np.float32)[:, None]
    return {"ident": np.eye(P, dtype=np.float32), "cos": np.cos(ang)[rows % half].astype(np.float32), "sin": (np.sin(ang)[rows % half] * sign).astype(np.float32)}


def kernel(**inputs):
    from concourse import bacc
    from concourse.bass_utils import run_bass_kernel_spmd

    def a(name):
        return np.asarray(inputs[name])

    def by_tile(v, n):
        return np.ascontiguousarray(v.reshape(n, P).T)

    arrays = dict(constants())
    arrays["x"], arrays["ctx"] = a("x"), a("ctx_1024")
    arrays["ctxT"] = np.ascontiguousarray(a("ctx_1024").transpose(0, 2, 1))
    arrays["condT"] = np.ascontiguousarray(a("cond_1024").T)
    for new, old in (("w_mod0", "W_mod"), ("w_qkv0", "W_qkv"), ("w_proj0", "W_proj"), ("w_qc0", "W_qc"), ("w_kvc0", "W_kvc"),
                     ("w_cproj0", "W_cproj"), ("w_up0", "W_mlp1"), ("w_down0", "W_mlp2"), ("b_mod0", "b_mod"), ("b_qkv0", "b_qkv"),
                     ("b_proj0", "b_proj"), ("b_kvc0", "b_kvc"), ("b_cproj0", "b_cproj"), ("b_down0", "b_mlp2")):
        arrays[new] = a("L0_xcond_" + old)
    for new, old in (("w_qkv1", "qkv_w"), ("w_proj1", "sa_out_w"), ("w_qc1", "q_w"), ("w_cproj1", "ca_out_w"), ("w_up1", "ffn_w1"),
                     ("w_down1", "ffn_w2"), ("w_ln0", "ln1_w"), ("w_ln1", "ln2_w"), ("w_ln2", "ln3_w")):
        arrays[new] = np.ascontiguousarray(a("L1_xcond_" + old).T)
    arrays["w_kvc1"] = np.ascontiguousarray(np.concatenate([a("L1_xcond_k_w").T, a("L1_xcond_v_w").T], axis=1))
    for i in range(SITES):
        arrays[f"b_ln{i}"] = a(f"L1_xcond_ln{i + 1}_b")
    arrays["b_down1"] = a("L1_xcond_ffn_b2")
    arrays["b_qk_cols"] = by_tile(a("L0_xcond_b_qkv")[0:2 * D], 2 * KT)
    arrays["b_qc_cols"] = by_tile(a("L0_xcond_b_qc"), KT)
    arrays["b_kc_cols"] = by_tile(a("L0_xcond_b_kvc")[0:D], KT)
    arrays["b_up0_cols"] = by_tile(a("L0_xcond_b_mlp1"), FT)
    arrays["b_up1_cols"] = by_tile(a("L1_xcond_ffn_b1"), FT)

    nc = bacc.Bacc("TRN2", target_bir_lowering=False, num_devices=1)
    ins = {name: nc.dram_tensor("in_" + name, v.shape, mybir.dt.from_np(v.dtype), kind="ExternalInput").ap()
           for name, v in arrays.items()}
    out = nc.dram_tensor("out", (B, N, D), F32, kind="ExternalOutput").ap()
    build(nc, ins, out)
    r = run_bass_kernel_spmd(nc, [{"in_" + name: v for name, v in arrays.items()}], core_ids=[0])
    return r.results[0]["out"]
```

```python
from contextlib import ExitStack

import numpy as np
import concourse.bass as bass
from concourse import mybir

F32 = mybir.dt.float32
BF16 = mybir.dt.bfloat16
ALU = mybir.AluOpType
ACT = mybir.ActivationFunctionType
AX = mybir.AxisListType

P = 128
B, N, D, NH = 8, 256, 256, 16
HD = D // NH
S = 77
F = 1024
KT = D // P
NT = N // P
FT = F // P
STREAMS = 2
ITERS = B // STREAMS
LAYERS = 2
SITES = 3
SCALE = HD ** -0.5
EPS = (1e-6, 1e-5)
HEADS_A_TILE = P // HD
QUAD = 4
PAIR = 2 * HD
QUADS_A_TILE = HEADS_A_TILE // QUAD
NORM_SITES = 5
TERMS = [(0, 0), (0, 1), (0, 2), (1, 0), (1, 1), (2, 0)]
PARTS = 3
RUNS = (((0, 3, 0, 0), (3, 2, 1, 0), (5, 1, 2, 0)), ((5, 1, 0, 1), (3, 2, 0, 1), (0, 3, 0, 1)))
TROWS = HD * len(TERMS)
MROWS = TROWS + 2
SELF, CROSS = 0, 1
AHEAD = 1
SITES_AHEAD = LAYERS * SITES

NORM_COL = {(0, 0): 0, (0, 2): 1, (1, 0): 2, (1, 1): 3, (1, 2): 4}
PRE = {(0, 0): 0, (0, 1): 1, (0, 2): 2, (1, 2): 3}


HEAD_ORDER = [d for pair in range(HD // 2) for d in (pair, pair + HD // 2)]
CHANNELS = [m * P + h * HD + d for m in range(KT) for d in HEAD_ORDER for h in range(HEADS_A_TILE)]


def site(l, i):
    return l * SITES + i


MERGE = (
    0, 1, 1, 1, 4, 4, 1, 1, 7, 12, 1, 5, 1, 1, 4, 3, 5, 2, 3, 1, 2, 4, 2, 2, 2, 1, 7, 1, 2, 1, 1, 2, 5, 2, 3, 6,
    2, 2, 2, 13, 2, 1, 2, 1, 12, 1, 2, 7, 3, 3, 10, 16, 2, 2, 2, 8, 10, 1, 2, 3, 4, 1, 5, 1, 2, 1, 1, 1, 1, 1,
    6, 2, 1, 3, 1, 8, 1, 2, 1, 5, 1, 2, 3, 5, 4, 1, 16, 1, 2, 3,
)


def plan():
    A, Z = 0, 1

    def scores(s, l, c):
        n = NH if c == SELF else NH // 2
        return [("scores", s, l, c, j) for j in range(n)] + [("nmax", s, l, c), ("maxima", s, l, c)]

    def attend(s, l, c):
        out = [("probs", s, l, c, 0)]
        for g in range(1, NH // QUAD):
            out += [("probs", s, l, c, g), ("pv", s, l, c, g - 1)]
            if g == QUADS_A_TILE + 1:
                out.append(("norm", s, l, c, 0))
        return out + [("pv", s, l, c, NH // QUAD - 1), ("norm", s, l, c, 1), ("proj", s, l, c), ("add", s, l, c)]

    def ln(s, l, i):
        return [("stats", s, l, i), ("xhat", s, l, i), ("ln", s, l, i)]

    begin = [[("load", s), ("stats", s, 0, 0), ("xhat", s, 0, 0), ("mod", s), ("ln", s, 0, 0), ("qkv", s, 0), ("split", s, 0, SELF)]
             for s in (A, Z)]
    begin[A] = [("load", A), ("context",)] + begin[A][1:] + [("ctx_t",), ("ctx_k", 0), ("ctx_v", 0)]

    def blocks(s):
        out = []
        for l in range(LAYERS):
            if l:
                out += ln(s, l, 0) + [("qkv", s, l), ("split", s, l, SELF)] + scores(s, l, SELF)
            out += attend(s, l, SELF) + ln(s, l, 1) + [("qc", s, l), ("split", s, l, CROSS)]
            if (s, l) == (A, 0):
                out += [("ctx_k", 1), ("ctx_v", 1)]
            out += scores(s, l, CROSS) + attend(s, l, CROSS) + ln(s, l, 2)
            out += [("up", s, l, j) for j in range(FT // 2)] + [("down", s, l), ("add", s, l, 2)]
        return out + [("store", s)]

    head = begin[A] + scores(A, 0, SELF)
    lists = [[(st, 0) for st in blocks(A)] + [(st, 1) for st in head],
             [(st, 0) for st in begin[Z] + scores(Z, 0, SELF) + blocks(Z)]]
    body = []
    for turn, count in enumerate(MERGE):
        mine = lists[turn % STREAMS]
        body += mine[:count]
        del mine[:count]
    assert not lists[A] and not lists[Z]
    return head, body


HEAD, BODY = plan()
FIRST = 1 + [st[0] for st in HEAD].index("xhat")
ITERATION = HEAD + [st for st, ahead in BODY if not ahead]

OWN, PROB = ((0, 1), (2, 3)), (4, 5)
OUTB = (6, 7)


class Uses:

    def __init__(self):
        self.of, self.per, self.turn = {}, {}, {}

    def give(self, pool, key):
        t = self.turn.get(pool, 0)
        self.turn[pool] = t + 1
        b = pool[t % len(pool)]
        n = self.per.get(b, 0)
        self.per[b] = n + 1
        self.of[key] = (b, n)


def assign():
    banks, probs = Uses(), Uses()
    for st in ITERATION:
        name = st[0]
        own = OWN[0] if name.startswith("ctx") or name == "context" else OWN[st[1]]
        if name == "ln":
            for k in range(KT):
                banks.give(own, (*st, k))
        elif name in ("ctx_t", "qc", "proj", "down", "up", "maxima", "ctx_v", "ctx_k", "scores"):
            banks.give(own, st)
        elif name == "qkv":
            for part in "vqk":
                banks.give(own, (*st, part))
        elif name == "probs":
            for u in range(QUAD if st[3] == SELF else QUAD // 2):
                banks.give(PROB, (*st, u))
            probs.give((0, 1), st[1:])
        elif name == "pv" and st[4] % QUADS_A_TILE == 0:
            half = st[4] // QUADS_A_TILE
            banks.give(OUTB[half:half + 1], ("out", *st[1:4], half))
    return banks, probs


BANKS, PROBS = assign()


def head_of(g, t):
    half, ab = g // 2, g % 2
    return half * HEADS_A_TILE + 2 * t + ab, half, half * QUAD + t, ab


def slot(h):
    return (h % HEADS_A_TILE) * KT + h // HEADS_A_TILE


def build(nc, ins, out):
    with ExitStack() as ctx:
        def sb(name, shape, dt=F32):
            return ctx.enter_context(nc.sbuf_tensor(name, shape, dt))

        def sem(name):
            return ctx.enter_context(nc.semaphore(name))

        def both(name):
            return [sem(f"{name}{s}") for s in range(STREAMS)]

        w_qkv = [sb(f"w_qkv{l}", [P, KT, 3 * D]) for l in range(LAYERS)]
        w_proj = [[sb(f"w_proj{l}{c}", [P, KT, D]) for c in range(2)] for l in range(LAYERS)]
        w_qc = [sb(f"w_qc{l}", [P, KT, D]) for l in range(LAYERS)]
        w_kvc = [sb(f"w_kvc{l}", [P, KT, 2 * D]) for l in range(LAYERS)]
        w_up = [sb(f"w_up{l}", [P, KT, F]) for l in range(LAYERS)]
        w_down = [sb(f"w_down{l}", [P, FT, D]) for l in range(LAYERS)]
        ident = sb("ident", [P, P])
        identb = sb("identb", [P, P], BF16)
        cos = sb("cos", [P, N])
        sin = sb("sin", [P, N])
        b_v = sb("b_v", [P, D])
        b_cproj = sb("b_cproj", [P, D])
        b_vc = sb("b_vc", [S, D])
        b_ffn = sb("b_ffn", [P, D])
        b_qk = sb("b_qk", [P, 2 * KT])
        b_qc = sb("b_qc", [P, KT])
        b_kc = sb("b_kc", [P, KT])
        b_up = [sb(f"b_up{l}", [P, FT]) for l in range(LAYERS)]
        ones = sb("ones", [P, 2, PAIR])
        minus_half = sb("minus_half", [P, NT])
        eps_tile = sb("eps_tile", [P, LAYERS, NT])
        spare = sb("spare", [P, 8])
        mod_all = sb("mod_all", [P, NORM_SITES * 2 * KT, B])
        silu = sb("silu", [P, 4, KT, B])
        per = range(STREAMS)
        x = [sb(f"x{s}", [P, NT, D]) for s in per]
        xhat = [sb(f"xhat{s}", [P, NT, D]) for s in per]
        rden = [xhat[s][:].rearrange("p t d -> p (t d)") for s in per]
        xT = [sb(f"xT{s}", [P, KT, N]) for s in per]
        hT = [sb(f"hT{s}", [P, FT, N]) for s in per]
        qk = [hT[s][:, 0:4, :] for s in per]
        rot = [hT[s][:, 4:8, :] for s in per]
        parts = [sb(f"parts{s}", [P, 3, 4, N], BF16) for s in per]
        stack = [sb(f"stack{s}", [P, 2, NH, N], BF16) for s in per]
        v = [sb(f"v{s}", [P, NT, NH // 2, 2 * PAIR]) for s in per]
        gates = [sb(f"gates{s}", [P, 4, D]) for s in per]
        mod = [sb(f"mod{s}", [P, NORM_SITES * 2 * KT]) for s in per]
        kc_stack = [[sb(f"kc_stack{l}{s}", [MROWS, NH, S], BF16) for s in per] for l in range(LAYERS)]
        vc = [[sb(f"vc{l}{s}", [S, NH // 2, 2 * PAIR]) for s in per] for l in range(LAYERS)]
        stats = [sb(f"stats{s}", [P, NT, 6]) for s in per]
        mv = [sb(f"mv{s}", [P, NT, 2]) for s in per]
        rstd = [sb(f"rstd{s}", [P, 2, NT]) for s in per]
        nmax = [sb(f"nmax{s}", [P, NT, NH]) for s in per]
        nparts = [sb(f"nparts{s}", [P, NT, 2, NH], BF16) for s in per]
        nT = [sb(f"nT{s}", [2 * NH, N], BF16) for s in per]
        probs = sb("probs", [P, 2, QUAD, NT * N])
        ctx_in = sb("ctx_in", [S, STREAMS, D])
        ctx_hat = sb("ctx_hat", [S, STREAMS, D])
        ctx_T = [sb(f"ctx_T{l}", [P, KT, STREAMS, S]) for l in range(LAYERS)]
        kc = sb("kc", [P, STREAMS, KT, S])
        kc_rot = sb("kc_rot", [P, STREAMS, KT, S])
        kc_parts = sb("kc_parts", [P, 3, STREAMS, KT, S], BF16)
        c_stats = sb("c_stats", [S, STREAMS, 6])
        c_mv = sb("c_mv", [S, STREAMS, 2])
        c_rstd = sb("c_rstd", [S, 2, STREAMS])
        w_mod = probs[:].rearrange("p a b c -> p (a b c)")[:, 0:KT * 6 * D].rearrange("p (k n) -> p k n", k=KT)
        w_ln = stack[0][:].rearrange("p a b c -> p (a b c)").bitcast(F32)[:, 0:KT * 6 * D].rearrange("p (k n) -> p k n", k=KT)
        c_rows = stack[1][:].rearrange("p a b c -> p (a b c)").bitcast(F32)[0:B, 0:12 * D]
        c_bias = hT[0][:].rearrange("p a b -> p (a b)")[0:B, 0:6 * D]
        c_bias1 = hT[1][:].rearrange("p a b -> p (a b)")[0:B, 0:6 * D]
        g_bias = parts[0][:].rearrange("p a b c -> p (a b c)").bitcast(F32)[0:B, 0:2 * D]
        g_rows = parts[1][:].rearrange("p a b c -> p (a b c)").bitcast(F32)[0:B, 0:4 * D]

        psum = ctx.enter_context(nc.psum_tensor("psum", [P, 8, 512], F32))
        qk_dram = [nc.dram_tensor(f"qk_dram{s}", [P, 3, 4 * N], BF16).ap() for s in per]
        kc_dram = nc.dram_tensor("kc_dram", [P, 3, STREAMS * KT * S], BF16).ap()
        g_dram = nc.dram_tensor("gates_dram", [B, 4 * D], F32).ap()

        bank_full = [sem(f"bank_full{b}") for b in range(8)]
        bank_read = [sem(f"bank_read{b}") for b in range(8)]
        probs_used = [sem(f"probs_used{b}") for b in range(2)]
        x_loaded, gates_loaded, stored = both("x_loaded"), both("gates_loaded"), both("stored")
        x_added, x_biased, mod_ready = both("x_added"), both("x_biased"), both("mod_ready")
        stats_done, mv_ready, var_eps, rstd_ready, xhat_ready = (
            both("stats_done"), both("mv_ready"), both("var_eps"), both("rstd_ready"), both("xhat_ready"))
        rope_rot, rope_cos, rope_sin, rope_done = both("rope_rot"), both("rope_cos"), both("rope_sin"), both("rope_done")
        parts_ready, rest_ready, stacked, rden_ready = both("parts_ready"), both("rest_ready"), both("stacked"), both("rden_ready")
        nmax_done, nhigh_done, nparts_ready, n_stacked = (
            both("nmax_done"), both("nhigh_done"), both("nparts_ready"), both("n_stacked"))
        ctx_loaded, ctxT_loaded = sem("ctx_loaded"), sem("ctxT_loaded")
        c_stats_done, c_mv_ready, c_var_eps, c_rstd_ready, ctx_hat_ready = (
            sem("c_stats_done"), sem("c_mv_ready"), sem("c_var_eps"), sem("c_rstd_ready"), sem("ctx_hat_ready"))
        kc_rotated, kc_cos, kc_sin, kc_roped, kc_parts_ready, kc_rest, kc_stacked = (
            sem("kc_rotated"), sem("kc_cos"), sem("kc_sin"), sem("kc_roped"), sem("kc_parts_ready"),
            sem("kc_rest"), sem("kc_stacked"))
        written = [[sem(f"written{s}{p}") for p in range(3)] for s in per]
        kc_written = [sem(f"kc_written{p}") for p in range(3)]
        mod_loads, small_loads, early_loads, w_loads = sem("mod_loads"), sem("small_loads"), sem("early_loads"), sem("w_loads")
        pro_exp, pro_dve, pro_pe, pro_free, pro_gates = (
            sem("pro_exp"), sem("pro_dve"), sem("pro_pe"), sem("pro_free"), sem("pro_gates"))
        identb_ready = sem("identb_ready")
        zeros_ready, consts_ready, mod_all_ready, stack_ones = sem("zeros_ready"), sem("consts_ready"), sem("mod_all_ready"), sem("stack_ones")

        def full(eng, it, key):
            b, n = BANKS.of[key]
            eng.wait_ge(bank_full[b], it * BANKS.per[b] + n + 1)
            return psum[:, b, :]

        def free(eng, it, key):
            b, n = BANKS.of[key]
            eng.wait_ge(bank_read[b], it * BANKS.per[b] + n + AHEAD)
            return psum[:, b, :]

        def fills(ins_, key):
            ins_.then_inc(bank_full[BANKS.of[key][0]], 1)

        def reads(ins_, key):
            ins_.then_inc(bank_read[BANKS.of[key][0]], 1)

        def brought(eng, it, key):
            b, n = BANKS.of[key]
            eng.wait_ge(bank_read[b], it * BANKS.per[b] + n + 1 + AHEAD)

        def carry_wait(n):
            nc.vector.tensor_copy(spare[:, n:n + 1], spare[:, 0:1])

        def event(l, c):
            return l * 2 + c

        def cols(ap):
            return ap.rearrange("(k p) n -> p k n", p=P)

        small = [
            (ident[:], ins["ident"]), (cos[:], ins["cos"]), (sin[:], ins["sin"]),
            (b_v[:], ins["b_qkv0"][2 * D:3 * D].partition_broadcast(P)),
            (b_cproj[:], ins["b_cproj0"][0:D].partition_broadcast(P)),
            (b_vc[:], ins["b_kvc0"][D:2 * D].partition_broadcast(S)),
            (b_ffn[:], ins["b_down1"][0:D].partition_broadcast(P)),
            (b_qk[:], ins["b_qk_cols"]), (b_qc[:], ins["b_qc_cols"]), (b_kc[:], ins["b_kc_cols"]),
            (b_up[0][:], ins["b_up0_cols"]), (b_up[1][:], ins["b_up1_cols"]),
        ]
        early = [(w_qkv[0][:], cols(ins["w_qkv0"])), (w_kvc[0][:], cols(ins["w_kvc0"]))]
        big = []
        for l in range(LAYERS):
            if l:
                big += [(w_qkv[l][:], cols(ins[f"w_qkv{l}"])), (w_kvc[l][:], cols(ins[f"w_kvc{l}"]))]
            big += [(w_qc[l][:], cols(ins[f"w_qc{l}"])), (w_proj[l][0][:], cols(ins[f"w_proj{l}"])),
                    (w_proj[l][1][:], cols(ins[f"w_cproj{l}"])), (w_up[l][:], cols(ins[f"w_up{l}"])),
                    (w_down[l][:], cols(ins[f"w_down{l}"]))]
        first = [(silu[:, 0, :, :], ins["condT"].rearrange("(k p) b -> p k b", p=P)),
                 (w_mod, cols(ins["w_mod0"])), (c_bias, ins["b_mod0"][0:6 * D].partition_broadcast(B)),
                 (g_bias[:, 0:D], ins["b_proj0"][0:D].partition_broadcast(B)),
                 (g_bias[:, D:2 * D], ins["b_down0"][0:D].partition_broadcast(B))]
        for i in range(SITES):
            first.append((w_ln[:, :, i * 2 * D:(i + 1) * 2 * D], cols(ins[f"w_ln{i}"])))
            first.append((c_bias1[:, i * 2 * D:(i + 1) * 2 * D], ins[f"b_ln{i}"][0:2 * D].partition_broadcast(B)))
        MOD_CHUNKS = 6

        block = ctx.enter_context(nc.Block())

        @block.sync
        def _(sp):
            def stage(it, st):
                def load(s):
                    sp.wait_ge(stored[s], (it + AHEAD) * 16)
                    sp.dma_start(x[s][:], ins["x"][it * STREAMS + s].rearrange("(t p) d -> p t d", p=P)).then_inc(x_loaded[s], 16)

                def load_gates(s):
                    sp.wait_ge(stored[s], (it + AHEAD) * 16)
                    sp.dma_start(gates[s][:], g_dram[it * STREAMS + s].partition_broadcast(P)).then_inc(gates_loaded[s], 16)

                def context():
                    sp.wait_ge(x_added[0], it * LAYERS * SITES + SITES_AHEAD)
                    for s in per:
                        sp.dma_start(ctx_in[:, s, :], ins["ctx"][it * STREAMS + s]).then_inc(ctx_loaded, 16)
                        sp.dma_start(ctx_T[1][:, :, s, :], ins["ctxT"][it * STREAMS + s].rearrange("(k p) n -> p k n", p=P)).then_inc(ctxT_loaded, 16)

                def through_dram(src, dram, ready, base, written, before, gather):
                    for part in range(3):
                        sp.wait_ge(ready, base + part + 1)
                        sp.dma_start(dram[:, part], src[:, part]).then_inc(written[part], 16)
                    for part in range(3):
                        sp.wait_ge(written[part], (before + 1) * 16)
                        gather(part)

                def blocks_of(run, tile, dram, at, w):
                    first, blocks, part, step = run
                    row, part_stride = dram.ap[0][0], dram.ap[1][0]
                    frm = bass.AP(dram.tensor, dram.offset + part * part_stride + at, [[step * part_stride, blocks], [row, P], [1, w]])
                    return tile[first * HD:(first + blocks) * HD].rearrange("d h n -> d (h n)"), frm

                def stack_q(s, l, c):
                    e = event(l, c)
                    n = 4 if c == SELF else 2

                    def gather(part):
                        for side in range(2 if c == SELF else 1):
                            dst, frm = blocks_of(RUNS[side][part], stack[s][:, side], qk_dram[s], side * KT * N, KT * N)
                            sp.dma_start(dst, frm).then_inc(stacked[s], 16)

                    through_dram(parts[s][:, :, 0:n, :].rearrange("p a m n -> p a (m n)"), qk_dram[s][:, :, 0:n * N],
                                 parts_ready[s], it * 12 + 3 * e, written[s], it * 4 + e, gather)

                def stack_kc(l):
                    for s in per:
                        sp.wait_ge(x_added[s], it * LAYERS * SITES + site(l, 1) + 1)
                    def gather(part):
                        for s in per:
                            dst, frm = blocks_of(RUNS[1][part], kc_stack[l][s], kc_dram, s * KT * S, KT * S)
                            sp.dma_start(dst, frm).then_inc(kc_stacked, 16)

                    through_dram(kc_parts[:].rearrange("p a s k n -> p a (s k n)"), kc_dram, kc_parts_ready, it * 6 + 3 * l + AHEAD,
                                 kc_written, it * LAYERS + l, gather)

                def stack_maxima(s, l, c):
                    brought(sp, it, ("maxima", s, l, c))
                    for part in range(2):
                        sp.dma_start(stack[s][TROWS + part:TROWS + part + 1, 0, :, :], nT[s][part * NH:(part + 1) * NH, :]).then_inc(n_stacked[s], 16)

                def store(s):
                    sp.wait_ge(x_added[s], (it + 1) * LAYERS * SITES + SITES_AHEAD)
                    sp.dma_start(out[it * STREAMS + s].rearrange("(t p) d -> p t d", p=P), x[s][:]).then_inc(stored[s], 16)

                if st[0] == "load":
                    load(st[1])
                elif st[0] == "mod":
                    load_gates(st[1])
                elif st[0] == "context":
                    context()
                elif st[0] == "split":
                    stack_q(*st[1:])
                elif st[0] == "ctx_k":
                    stack_kc(st[1])
                elif st[0] == "maxima":
                    stack_maxima(*st[1:])
                elif st[0] == "store":
                    store(st[1])

            for st in HEAD[:FIRST]:
                stage(0, st)
            for dst, src in first:
                sp.dma_start(dst, src).then_inc(mod_loads, 16)
            for dst, src in small:
                sp.dma_start(dst, src).then_inc(small_loads, 16)
            for dst, src in early:
                sp.dma_start(dst, src).then_inc(early_loads, 16)
            for dst, src in big:
                sp.dma_start(dst, src).then_inc(w_loads, 16)
            sp.wait_ge(pro_gates, 1)
            sp.dma_start(g_dram, g_rows).then_inc(pro_free, 16)
            sp.wait_ge(pro_free, 16)
            sp.wait_ge(mod_all_ready, 1)
            for st in HEAD[FIRST:]:
                stage(0, st)
            with sp.Fori(0, ITERS - 1) as it:
                for st, ahead in BODY:
                    stage(it + 1 if ahead else it, st)
            for st, ahead in BODY:
                if not ahead:
                    stage(ITERS - 1, st)
            for s in per:
                sp.wait_ge(stored[s], (ITERS + AHEAD) * 16)

        @block.gpsimd
        def _(pool):
            g = nc.gpsimd
            pool.wait_ge(consts_ready, 1)
            def stage(it, st):
                def modulation(s):
                    pool.wait_ge(x_added[s], it * LAYERS * SITES + SITES_AHEAD)
                    g.tensor_copy(mod[s][:], mod_all[:, :, it * STREAMS + s]).then_inc(mod_ready[s], 1)

                def inv_std(mv_, r, ready, eps_done, done, e, per_it, eps, n):
                    pool.wait_ge(ready, it * per_it + e + 1)
                    g.tensor_tensor(r[:, 0, :], mv_[:, :, 1], eps, ALU.add).then_inc(eps_done, 1)
                    pool.wait_ge(eps_done, it * per_it + e + 1)
                    g.tensor_tensor(r[:, 1, :], r[:, 0, :], minus_half[0:n, :], ALU.pow).then_inc(done, 1)

                def ln_std(s, l, i):
                    inv_std(mv[s], rstd[s], mv_ready[s], var_eps[s], rstd_ready[s], site(l, i), LAYERS * SITES, eps_tile[:, l, :], P)

                def add_bias(s, l, i):
                    if (l, i) in PRE:
                        pool.wait_ge(xhat_ready[s], it * LAYERS * SITES + site(l, i) + 1)
                        if (l, i) == (0, 0):
                            pool.wait_ge(gates_loaded[s], (it + 1) * 16)
                        bias = {(0, 0): gates[s][:, 1, :], (0, 1): b_cproj[:], (0, 2): gates[s][:, 3, :], (1, 2): b_ffn[:]}[(l, i)]
                        for t in range(NT):
                            last = g.tensor_tensor(x[s][:, t, :], x[s][:, t, :], bias, ALU.add)
                        last.then_inc(x_biased[s], 1)

                def rope(s, l, c):
                    if l == 1:
                        n = 4 if c == SELF else 2
                        pool.wait_ge(rope_rot[s], it * 2 + c + 1)
                        for m in range(n):
                            last = g.tensor_tensor(qk[s][:, m, :], qk[s][:, m, :], cos[:], ALU.mult)
                        last.then_inc(rope_cos[s], 1)

                if st[0] == "mod":
                    modulation(st[1])
                    add_bias(st[1], 0, 0)
                elif st[0] == "context":
                    inv_std(c_mv, c_rstd, c_mv_ready, c_var_eps, c_rstd_ready, 0, 1, eps_tile[0:S, 0, :], S)
                elif st[0] == "stats":
                    ln_std(*st[1:])
                elif st[0] == "xhat" and site(*st[2:]):
                    add_bias(*st[1:])
                elif st[0] == "split":
                    rope(*st[1:])

            for st in HEAD[:FIRST]:
                stage(0, st)
            pool.wait_ge(small_loads, 16 * len(small))
            pool.wait_ge(mod_all_ready, 1)
            for st in HEAD[FIRST:]:
                stage(0, st)
            with pool.Fori(0, ITERS - 1) as it:
                for st, ahead in BODY:
                    stage(it + 1 if ahead else it, st)
            for st, ahead in BODY:
                if not ahead:
                    stage(ITERS - 1, st)

        @block.scalar
        def _(act):
            a = nc.scalar
            act.wait_ge(mod_loads, 16 * len(first))
            a.activation(silu[:, 1], silu[:, 0], ACT.Exp, scale=-1.0).then_inc(pro_exp, 1)
            act.wait_ge(small_loads, 16 * len(small))
            def stage(it, st):
                def ln(s, l, i):
                    if (l, i) == (0, 0):
                        act.wait_ge(mod_ready[s], it + 1)
                    for k in range(KT):
                        ps = full(act, it, ("ln", s, l, i, k))
                        if (l, i) in NORM_COL:
                            col = NORM_COL[(l, i)] * 2 * KT
                            out_ = a.activation(xT[s][:, k, :], ps[:, 0:N], ACT.Identity,
                                                scale=mod[s][:, col + k:col + k + 1],
                                                bias=mod[s][:, col + KT + k:col + KT + k + 1])
                        else:
                            out_ = a.activation(xT[s][:, k, :], ps[:, 0:N], ACT.Copy)
                        reads(out_, ("ln", s, l, i, k))

                def q_out(s, l, c):
                    for part in ("q", "k") if c == SELF else ("q",):
                        key = ("qkv", s, l, part) if c == SELF else ("qc", s, l)
                        ps = full(act, it, key)
                        m0 = 0 if part == "q" else KT
                        if l == 0:
                            bias = b_qk if c == SELF else b_qc
                            for m in range(KT):
                                last = a.activation(qk[s][:, m0 + m, :], ps[:, m * N:(m + 1) * N], ACT.Identity,
                                                    bias=bias[:, m0 + m:m0 + m + 1])
                        else:
                            last = a.activation(qk[s][:, m0:m0 + KT, :].rearrange("p m n -> p (m n)"), ps, ACT.Copy)
                        reads(last, key)

                def ctx_t():
                    ps = full(act, it, ("ctx_t",))
                    reads(a.activation(ctx_T[0][:].rearrange("p k s n -> p (k s n)"), ps[:, 0:KT * STREAMS * S], ACT.Copy), ("ctx_t",))

                def kc_out(l):
                    ps = full(act, it, ("ctx_k", l))
                    act.wait_ge(kc_parts_ready, it * 6 + l * 3 + AHEAD)
                    for m in range(KT):
                        src = ps[:, m * STREAMS * S:(m + 1) * STREAMS * S].rearrange("p (s n) -> p s n", s=STREAMS)
                        if l == 0:
                            last = a.activation(kc[:, :, m, :], src, ACT.Identity, bias=b_kc[:, m:m + 1])
                        else:
                            last = a.activation(kc[:, :, m, :], src, ACT.Copy)
                    reads(last, ("ctx_k", l))

                def maxima(s, l, c):
                    ps = full(act, it, ("maxima", s, l, c))
                    src = ps[0:2 * NH, 0:N // 2].bitcast(BF16)
                    reads(a.activation(nT[s][:], src, ACT.Copy), ("maxima", s, l, c))

                def exps(s, l, c, g):
                    buf, n = PROBS.of[(s, l, c, g)]
                    act.wait_ge(probs_used[buf], it * PROBS.per[buf] + n + AHEAD)
                    for u in range(QUAD if c == SELF else QUAD // 2):
                        key = ("probs", s, l, c, g, u)
                        ps = full(act, it, key)
                        if c == SELF:
                            last = a.activation(probs[:, buf, u, :], ps, ACT.Exp, scale=SCALE)
                        else:
                            last = a.activation(probs[0:S, buf, 2 * u:2 * u + 2, 0:N],
                                                ps[0:S, :].rearrange("p (h n) -> p h n", h=2), ACT.Exp, scale=SCALE)
                        reads(last, key)

                def gelu(s, l, j):
                    ps = full(act, it, ("up", s, l, j))
                    fn = ACT.Gelu_apprx_tanh if l == 0 else ACT.Gelu
                    for m in range(2):
                        f = 2 * j + m
                        last = a.activation(hT[s][:, f, :], ps[:, m * N:(m + 1) * N], fn, bias=b_up[l][:, f:f + 1])
                    reads(last, ("up", s, l, j))

                if st[0] == "ln":
                    ln(*st[1:])
                elif st[0] == "qkv":
                    q_out(st[1], st[2], SELF)
                elif st[0] == "qc":
                    q_out(st[1], st[2], CROSS)
                elif st[0] == "ctx_t":
                    ctx_t()
                elif st[0] == "ctx_k":
                    kc_out(st[1])
                elif st[0] == "maxima":
                    maxima(*st[1:])
                elif st[0] == "probs":
                    exps(*st[1:])
                elif st[0] == "up":
                    gelu(*st[1:])

            for st in HEAD:
                stage(0, st)
            with act.Fori(0, ITERS - 1) as it:
                for st, ahead in BODY:
                    stage(it + 1 if ahead else it, st)
            for st, ahead in BODY:
                if not ahead:
                    stage(ITERS - 1, st)

        @block.vector
        def _(dve):
            d = nc.vector
            def stage(it, st):
                def moments(src, st_, mv_, sems, e, per_it, who):
                    done, mvr = sems
                    for t in range(2):
                        last = d.bn_stats(st_[:, t, :], src[:, t, :])
                    last.then_inc(done, 1)
                    dve.wait_ge(done, it * per_it + e + 1)
                    carry_wait(who)
                    for t in range(2):
                        last = d.bn_aggr(mv_[:, t, :], st_[:, t, :])
                    last.then_inc(mvr, 1)

                def normalise(src, mv_, r, dst, sems, e, per_it):
                    mvr, eps_ready, ready = sems
                    dve.wait_ge(mvr, it * per_it + e + 1)
                    dve.wait_ge(eps_ready, it * per_it + e + 1)
                    for t in range(2):
                        last = d.tensor_scalar(dst[:, t, :], src[:, t, :], mv_[:, t, 0:1], r[:, 1, t:t + 1], ALU.subtract, ALU.mult)
                    last.then_inc(ready, 1)

                def ln_stats(s, l, i):
                    e = site(l, i)
                    if e == 0:
                        dve.wait_ge(x_loaded[s], (it + 1) * 16)
                    else:
                        dve.wait_ge(x_added[s], it * LAYERS * SITES + e + SITES_AHEAD)
                    moments(x[s], stats[s], mv[s], (stats_done[s], mv_ready[s]), e, LAYERS * SITES, 1 + s)

                def ln_xhat(s, l, i):
                    normalise(x[s], mv[s], rstd[s], xhat[s], (mv_ready[s], rstd_ready[s], xhat_ready[s]), site(l, i), LAYERS * SITES)

                def context():
                    dve.wait_ge(ctx_loaded, (it + 1) * 16 * STREAMS)
                    moments(ctx_in, c_stats, c_mv, (c_stats_done, c_mv_ready), 0, 1, 3)
                    normalise(ctx_in, c_mv, c_rstd, ctx_hat, (c_mv_ready, c_rstd_ready, ctx_hat_ready), 0, 1)

                def split(src, n, dst, rest_sem, ready, base_rest, base_ready):
                    d.tensor_copy(dst[0], src).then_inc(ready, 1)
                    dve.wait_ge(ready, base_ready + 1)
                    d.tensor_tensor(src, src, dst[0], ALU.subtract).then_inc(rest_sem, 1)
                    dve.wait_ge(rest_sem, base_rest + 1)
                    d.tensor_copy(dst[1], src).then_inc(ready, 1)
                    dve.wait_ge(ready, base_ready + 2)
                    d.tensor_tensor(dst[2], src, dst[1], ALU.subtract).then_inc(ready, 1)

                SWAP = [i ^ (HD // 2) for i in range(32)]

                def split_q(s, l, c):
                    n = 4 if c == SELF else 2
                    brought(dve, it, ("qkv", s, l, "k") if c == SELF else ("qc", s, l))
                    if l == 1:
                        carry_wait(4 + s)
                    src = qk[s][:, 0:n, :]
                    if l == 1:
                        e = it * 2 + c + 1
                        turned = rot[s][:, 0:n, :]
                        d.stream_shuffle(turned, src, SWAP).then_inc(rope_rot[s], 1)
                        dve.wait_ge(rope_rot[s], e)
                        d.tensor_tensor(turned, turned, sin[:].unsqueeze(1).to_broadcast([P, n, N]), ALU.mult).then_inc(rope_sin[s], 1)
                        dve.wait_ge(rope_sin[s], e)
                        dve.wait_ge(rope_cos[s], e)
                        d.tensor_tensor(src, src, turned, ALU.add).then_inc(rope_done[s], 1)
                        dve.wait_ge(rope_done[s], e)
                    ev = event(l, c)
                    split(src, n, [parts[s][:, p, 0:n, :] for p in range(3)], rest_ready[s], parts_ready[s],
                          it * 4 + ev, it * 12 + 3 * ev)

                def v_out(ps, dst, bias, n):
                    to = bass.AP(dst.tensor, dst.offset, [dst.ap[0], [2 * PAIR, NH // 2], [PAIR + HD, 2], [1, HD]])
                    frm = ps.rearrange("p (h a d) -> p h a d", a=2, d=HD)
                    if bias is None:
                        return d.tensor_copy(to, frm)
                    return d.tensor_tensor(to, frm, bias.rearrange("p (h a d) -> p h a d", a=2, d=HD), ALU.add)

                def self_v(s, l):
                    key = ("qkv", s, l, "v")
                    ps = full(dve, it, key)
                    for t in range(NT):
                        last = v_out(ps[:, t * D:(t + 1) * D], v[s][:, t], b_v[:] if l == 0 else None, P)
                    reads(last, key)

                def ctx_v(l):
                    key = ("ctx_v", l)
                    for s in per:
                        dve.wait_ge(x_added[s], it * LAYERS * SITES + site(l, 1) + 1)
                    ps = full(dve, it, key)
                    for s in per:
                        last = v_out(ps[0:S, s * D:(s + 1) * D], vc[l][s][:], b_vc[:] if l == 0 else None, S)
                    reads(last, key)

                def ctx_k(l):
                    brought(dve, it, ("ctx_k", l))
                    if l == 1:
                        carry_wait(6)
                    src = kc[:].rearrange("p s k n -> p (s k) n")
                    if l == 1:
                        turned = kc_rot[:].rearrange("p s k n -> p (s k) n")
                        wide = [P, STREAMS * KT, S]
                        d.stream_shuffle(turned, src, SWAP).then_inc(kc_rotated, 1)
                        dve.wait_ge(kc_rotated, it + 1)
                        d.tensor_tensor(turned, turned, sin[:, 0:S].unsqueeze(1).to_broadcast(wide), ALU.mult).then_inc(kc_sin, 1)
                        d.tensor_tensor(src, src, cos[:, 0:S].unsqueeze(1).to_broadcast(wide), ALU.mult).then_inc(kc_cos, 1)
                        dve.wait_ge(kc_sin, it + 1)
                        dve.wait_ge(kc_cos, it + 1)
                        d.tensor_tensor(src, src, turned, ALU.add).then_inc(kc_roped, 1)
                        dve.wait_ge(kc_roped, it + 1)
                    dve.wait_ge(kc_stacked, 16 * AHEAD + (it * LAYERS + l) * 16 * PARTS * STREAMS)
                    split(src, None, [kc_parts[:, p].rearrange("p s k n -> p (s k) n") for p in range(3)], kc_rest, kc_parts_ready,
                          it * LAYERS + l, it * 6 + 3 * l + AHEAD)

                def row_max(s, l, c, j):
                    key = ("scores", s, l, c, j)
                    ps = full(dve, it, key)
                    if c == SELF:
                        last = d.tensor_reduce(nmax[s][:, :, slot(j)], ps.rearrange("p (t n) -> p t n", t=NT), AX.X, ALU.max, negate=True)
                    else:
                        for h in range(2):
                            src = ps[:, h * 2 * P:(h + 1) * 2 * P].rearrange("p (t n) -> p t n", t=NT)[:, :, 0:S]
                            last = d.tensor_reduce(nmax[s][:, :, slot(2 * j + h)], src, AX.X, ALU.max, negate=True)
                    reads(last, key)

                def maxima(s, l, c):
                    e = it * 4 + event(l, c) + 1
                    last_j = (NH if c == SELF else NH // 2) - 1
                    brought(dve, it, ("scores", s, l, c, last_j))
                    d.tensor_copy(nparts[s][:, :, 0, :], nmax[s][:]).then_inc(nhigh_done[s], 1)
                    dve.wait_ge(nhigh_done[s], e)
                    d.tensor_tensor(nparts[s][:, :, 1, :], nmax[s][:], nparts[s][:, :, 0, :], ALU.subtract).then_inc(nparts_ready[s], 1)

                def norm(s, l, c, half):
                    key = ("out", s, l, c, half)
                    buf, n = PROBS.of[(s, l, c, (half + 1) * QUADS_A_TILE - 1)]
                    dve.wait_ge(probs_used[buf], it * PROBS.per[buf] + n + 1 + AHEAD)
                    ps = psum[:, OUTB[half], :]
                    inv = rden[s][:, half * N:(half + 1) * N]
                    d.reciprocal(inv, ps[:, N:2 * N]).then_inc(rden_ready[s], 1)
                    dve.wait_ge(rden_ready[s], it * 4 * KT + event(l, c) * KT + half + 1)
                    reads(d.tensor_tensor(xT[s][:, half, :], ps[:, 0:N], inv, ALU.mult), key)

                def residual(s, l, i, key):
                    ps = full(dve, it, key).rearrange("p (t n) -> p t n", t=NT)
                    if (l, i) in PRE:
                        dve.wait_ge(x_biased[s], it * len(PRE) + PRE[(l, i)] + 1)
                    if l == 0 and i != 1:
                        gate = gates[s][:, 0 if i == 0 else 2, :].unsqueeze(1).to_broadcast([P, NT, D])
                        dve.wait_ge(gates_loaded[s], (it + 1) * 16)
                        reads(d.tensor_tensor(xhat[s][:], ps, gate, ALU.mult), key)
                        brought(dve, it, key)
                        d.tensor_tensor(x[s][:], x[s][:], xhat[s][:], ALU.add).then_inc(x_added[s], 1)
                        return
                    d.tensor_tensor(x[s][:], ps, x[s][:], ALU.add).then_inc(bank_read[BANKS.of[key][0]], 1)
                    brought(dve, it, key)
                    d.nop().then_inc(x_added[s], 1)

                if st[0] == "context":
                    context()
                elif st[0] == "stats":
                    ln_stats(*st[1:])
                elif st[0] == "xhat":
                    ln_xhat(*st[1:])
                elif st[0] == "qkv":
                    self_v(st[1], st[2])
                elif st[0] == "split":
                    split_q(*st[1:])
                elif st[0] == "ctx_k":
                    ctx_k(st[1])
                elif st[0] == "ctx_v":
                    ctx_v(st[1])
                elif st[0] == "scores":
                    row_max(*st[1:])
                elif st[0] == "nmax":
                    maxima(*st[1:])
                elif st[0] == "norm":
                    norm(*st[1:])
                elif st[0] == "add":
                    _, s, l, i = st
                    residual(s, l, i, ("down", s, l) if i == 2 else ("proj", s, l, i))

            for sem_ in bank_read + probs_used + [kc_parts_ready]:
                dve.sem_inc(sem_, AHEAD)
            for sem_ in x_added:
                dve.sem_inc(sem_, SITES_AHEAD)
            for sem_ in stored + [kc_stacked]:
                dve.sem_inc(sem_, 16 * AHEAD)
            d.memset(minus_half[:], -0.5)
            for l in range(LAYERS):
                d.memset(eps_tile[:, l], EPS[l])
            d.memset(spare[:], 0.0).then_inc(consts_ready, 1)
            d.memset(ones[:], 0.0).then_inc(zeros_ready, 1)
            for s in per:
                d.memset(v[s][:], 0.0)
                for l in range(LAYERS):
                    d.memset(vc[l][s][:], 0.0)
                    d.memset(kc_stack[l][s][TROWS:MROWS], 1.0)
            d.memset(stack[1][TROWS:MROWS, 1], 1.0)
            dve.wait_ge(zeros_ready, 1)
            for n in range(2):
                last = d.memset(ones[:, n, n * HD:(n + 1) * HD], 1.0)
            last.then_inc(consts_ready, 1)
            dve.wait_ge(pro_exp, 1)
            d.tensor_scalar(silu[:, 2], silu[:, 1], 1.0, None, ALU.add).then_inc(pro_dve, 1)
            dve.wait_ge(pro_dve, 1)
            d.reciprocal(silu[:, 1], silu[:, 2]).then_inc(pro_dve, 1)
            dve.wait_ge(pro_dve, 2)
            d.tensor_tensor(silu[:, 3], silu[:, 0], silu[:, 1], ALU.mult).then_inc(pro_dve, 1)
            for st in HEAD[:FIRST]:
                stage(0, st)
            bias_rows = [c_bias, c_bias1]
            for n in range(MOD_CHUNKS):
                dve.wait_ge(pro_pe, n + 1)
                bias = bias_rows[n // 3][:, (n % 3) * 512:(n % 3) * 512 + 512]
                d.tensor_tensor(c_rows[:, n * 512:(n + 1) * 512], psum[0:B, n, :], bias, ALU.add).then_inc(pro_dve, 1)
            d.memset(stack[0][TROWS:MROWS, 1], 1.0).then_inc(stack_ones, 1)
            dve.wait_ge(pro_dve, 3 + MOD_CHUNKS)
            gate_at = (2 * D, 5 * D)
            scale_at = (D, 4 * D, 6 * D, 8 * D, 10 * D)
            shift_at = (0, 3 * D, 7 * D, 9 * D, 11 * D)
            for at in scale_at:
                last = d.tensor_scalar(c_rows[:, at:at + D], c_rows[:, at:at + D], 1.0, None, ALU.add)
            last.then_inc(pro_dve, 1)
            for n, at in enumerate(gate_at):
                d.tensor_copy(g_rows[:, 2 * n * D:(2 * n + 1) * D], c_rows[:, at:at + D])
                last = d.tensor_tensor(g_rows[:, (2 * n + 1) * D:(2 * n + 2) * D], c_rows[:, at:at + D], g_bias[:, n * D:(n + 1) * D], ALU.mult)
            last.then_inc(pro_gates, 1)
            dve.wait_ge(pro_pe, MOD_CHUNKS + 1)
            d.tensor_copy(mod_all[:], psum[:, 7, 0:NORM_SITES * 2 * KT * B].rearrange("p (c b) -> p c b", b=B)).then_inc(mod_all_ready, 1)
            dve.wait_ge(small_loads, 16 * len(small))
            d.tensor_copy(identb[:], ident[:]).then_inc(identb_ready, 1)
            dve.wait_ge(consts_ready, 2)
            for st in HEAD[FIRST:]:
                stage(0, st)
            with dve.Fori(0, ITERS - 1) as it:
                for st, ahead in BODY:
                    stage(it + 1 if ahead else it, st)
            for st, ahead in BODY:
                if not ahead:
                    stage(ITERS - 1, st)

        @block.tensor
        def _(pe):
            t_ = nc.tensor

            def group(out_, pairs):
                for n, (lhsT, rhs) in enumerate(pairs):
                    last = t_.matmul(out_, lhsT, rhs, start=(n == 0), stop=(n == len(pairs) - 1))
                return last

            pe.wait_ge(mod_loads, 16 * len(first))
            pe.wait_ge(pro_dve, 3)
            for n in range(MOD_CHUNKS):
                w = (w_mod if n < 3 else w_ln)[:, :, (n % 3) * 512:(n % 3) * 512 + 512]
                row = 3 if n < 3 else 0
                group(psum[0:B, n, :], [(silu[:, row, k, :], w[:, k, :]) for k in range(KT)]).then_inc(pro_pe, 1)
            pe.wait_ge(small_loads, 16 * len(small))
            pe.wait_ge(pro_dve, 4 + MOD_CHUNKS)
            scale_at = (D, 4 * D, 6 * D, 8 * D, 10 * D)
            shift_at = (0, 3 * D, 7 * D, 9 * D, 11 * D)
            for n in range(NORM_SITES):
                for m, at in enumerate((scale_at[n], shift_at[n])):
                    for k in range(KT):
                        col = ((n * 2 + m) * KT + k) * B
                        last = t_.transpose(psum[:, 7, col:col + B], c_rows[:, at + k * P:at + (k + 1) * P], ident[0:B, 0:B])
            last.then_inc(pro_pe, 1)
            pe.wait_ge(mod_all_ready, 1)
            pe.wait_ge(stack_ones, 1)
            pe.wait_ge(identb_ready, 1)
            pe.wait_ge(early_loads, 16 * len(early))
            def stage(it, st):
                def ln(s, l, i):
                    pe.wait_ge(xhat_ready[s], it * LAYERS * SITES + site(l, i) + 1)
                    for k in range(KT):
                        key = ("ln", s, l, i, k)
                        ps = free(pe, it, key)
                        for t in range(NT):
                            last = t_.transpose(ps[:, t * P:(t + 1) * P], xhat[s][:, t, k * P:(k + 1) * P], ident[:])
                        fills(last, key)

                def project(key, w, at, s, after=None):
                    ps = free(pe, it, key)
                    for m in range(KT):
                        for k in range(KT):
                            if after and m == 0:
                                brought(pe, it, (*after, k))
                            last = t_.matmul(ps[:, m * N:(m + 1) * N], w[:, k, at + m * P:at + (m + 1) * P], xT[s][:, k, :],
                                             start=(k == 0), stop=(k == KT - 1))
                    fills(last, key)

                def qkv(s, l):
                    key = ("qkv", s, l, "v")
                    ps = free(pe, it, key)
                    for t in range(NT):
                        for k in range(KT):
                            if t == 0:
                                brought(pe, it, ("ln", s, l, 0, k))
                            last = t_.matmul(ps[:, t * D:(t + 1) * D], xT[s][:, k, t * P:(t + 1) * P], w_qkv[l][:, k, 2 * D:3 * D],
                                             start=(k == 0), stop=(k == KT - 1))
                    fills(last, key)
                    project(("qkv", s, l, "q"), w_qkv[l], 0, s)
                    project(("qkv", s, l, "k"), w_qkv[l], D, s)

                def ctx_t():
                    pe.wait_ge(ctx_hat_ready, it + 1)
                    ps = free(pe, it, ("ctx_t",))
                    for k in range(KT):
                        for s in per:
                            at = (k * STREAMS + s) * S
                            last = t_.transpose(ps[:, at:at + S], ctx_hat[:, s, k * P:(k + 1) * P], ident[0:S, 0:S])
                    fills(last, ("ctx_t",))

                def ctx_ready(l):
                    if l == 0:
                        brought(pe, it, ("ctx_t",))
                    else:
                        pe.wait_ge(ctxT_loaded, (it + 1) * 16 * STREAMS)

                def ctx_k(l):
                    ctx_ready(l)
                    key = ("ctx_k", l)
                    ps = free(pe, it, key)
                    w = STREAMS * S
                    for m in range(KT):
                        last = group(ps[:, m * w:(m + 1) * w], [(w_kvc[l][:, k, m * P:(m + 1) * P], ctx_T[l][:, k].rearrange("p s n -> p (s n)")) for k in range(KT)])
                    fills(last, key)

                def ctx_v(l):
                    ctx_ready(l)
                    key = ("ctx_v", l)
                    ps = free(pe, it, key)
                    for s in per:
                        last = group(ps[0:S, s * D:(s + 1) * D], [(ctx_T[l][:, k, s, :], w_kvc[l][:, k, D:2 * D]) for k in range(KT)])
                    fills(last, key)

                def q_stacked(s, l, c):
                    pe.wait_ge(stacked[s], (it * LAYERS * 3 + 3 * l + (2 if c == SELF else 3)) * PARTS * 16)
                    if c == CROSS:
                        pe.wait_ge(kc_stacked, 16 * AHEAD + (it * LAYERS + l + 1) * 16 * PARTS * STREAMS)

                def scores(s, l, c, j):
                    key = ("scores", s, l, c, j)
                    if j == 0:
                        q_stacked(s, l, c)
                    ps = free(pe, it, key)
                    for h in ([j] if c == SELF else [2 * j, 2 * j + 1]):
                        for t in range(NT):
                            q = stack[s][0:TROWS, 0, slot(h), t * P:(t + 1) * P]
                            if c == SELF:
                                last = t_.matmul(ps[:, t * N:(t + 1) * N], q, stack[s][0:TROWS, 1, slot(h), :], start=True, stop=True)
                            else:
                                at = (h % 2) * 2 * P + t * P
                                last = t_.matmul(ps[:, at:at + S], q, kc_stack[l][s][0:TROWS, slot(h), :], start=True, stop=True)
                    fills(last, key)

                def maxima(s, l, c):
                    key = ("maxima", s, l, c)
                    pe.wait_ge(nparts_ready[s], it * 4 + event(l, c) + 1)
                    ps = free(pe, it, key)[0:2 * NH, 0:N // 2].bitcast(BF16)
                    for t in range(NT):
                        last = t_.transpose(ps[:, t * P:(t + 1) * P], nparts[s][:, t].rearrange("p a h -> p (a h)"), identb[:])
                    fills(last, key)

                def probs_(s, l, c, g):
                    if g == 0:
                        pe.wait_ge(n_stacked[s], (it * 4 + event(l, c) + 1) * 32)
                    for u in range(QUAD if c == SELF else QUAD // 2):
                        key = ("probs", s, l, c, g, u)
                        ps = free(pe, it, key)
                        if c == SELF:
                            h = head_of(g, u)[0]
                            q = stack[s][0:MROWS, 0, slot(h), :]
                            for t in range(NT):
                                last = t_.matmul(ps[:, t * N:(t + 1) * N], stack[s][0:MROWS, 1, slot(h), t * P:(t + 1) * P], q, start=True, stop=True)
                        else:
                            for w in range(2):
                                h = head_of(g, 2 * u + w)[0]
                                last = t_.matmul(ps[0:S, w * N:(w + 1) * N], kc_stack[l][s][:, slot(h), :], stack[s][0:MROWS, 0, slot(h), :], start=True, stop=True)
                        fills(last, key)

                def pv(s, l, c, g):
                    buf = PROBS.of[(s, l, c, g)][0]
                    half = g // QUADS_A_TILE
                    if g % QUADS_A_TILE == 0:
                        free(pe, it, ("out", s, l, c, half))
                    if g == 0:
                        brought(pe, it, ("qkv", s, l, "v") if c == SELF else ("ctx_v", l))
                    brought(pe, it, ("probs", s, l, c, g, (QUAD if c == SELF else QUAD // 2) - 1))
                    keys = NT if c == SELF else 1
                    for kind in range(2):
                        for k in range(keys):
                            for t in range(QUAD):
                                _, _, pair, ab = head_of(g, t)
                                if c == SELF:
                                    p = probs[:, buf, t, k * N:(k + 1) * N]
                                    w = v[s][:, k, pair, ab * PAIR:(ab + 1) * PAIR]
                                    one = ones[:, ab, :]
                                else:
                                    p = probs[0:S, buf, t, 0:N]
                                    w = vc[l][s][:, pair, ab * PAIR:(ab + 1) * PAIR]
                                    one = ones[0:S, ab, :]
                                rows = slice(t * PAIR, (t + 1) * PAIR)
                                last = t_.matmul(psum[rows, OUTB[half], kind * N:(kind + 1) * N], w if kind == 0 else one, p,
                                                 start=(kind == 0 and ab == 0 and k == 0), stop=(ab == 1 and k == keys - 1),
                                                 tile_position=(0, t * PAIR), skip_group_check=True)
                    last.then_inc(probs_used[buf], 1)

                def proj(s, l, c):
                    key = ("proj", s, l, c)
                    ps = free(pe, it, key)
                    for k in range(KT):
                        brought(pe, it, ("out", s, l, c, k))
                        for t in range(NT):
                            last = t_.matmul(ps[:, t * D:(t + 1) * D], xT[s][:, k, t * P:(t + 1) * P], w_proj[l][c][:, k, :],
                                             start=(k == 0 and t == 0), stop=(k == KT - 1), skip_group_check=True)
                    fills(last, key)

                def up(s, l, j):
                    project(("up", s, l, j), w_up[l], j * KT * P, s, ("ln", s, l, 2) if j == 0 else None)

                def down(s, l):
                    key = ("down", s, l)
                    ps = free(pe, it, key)
                    for t in range(NT):
                        for f in range(FT):
                            if t == 0 and f % 2 == 0:
                                brought(pe, it, ("up", s, l, f // 2))
                            last = t_.matmul(ps[:, t * D:(t + 1) * D], hT[s][:, f, t * P:(t + 1) * P], w_down[l][:, f, :],
                                             start=(f == 0), stop=(f == FT - 1))
                    fills(last, key)

                if st[0] == "ln":
                    ln(*st[1:])
                elif st[0] == "qkv":
                    qkv(*st[1:])
                elif st[0] == "qc":
                    project(st, w_qc[st[2]], 0, st[1], ("ln", st[1], st[2], 1))
                elif st[0] == "ctx_t":
                    ctx_t()
                elif st[0] == "ctx_k":
                    ctx_k(st[1])
                elif st[0] == "ctx_v":
                    ctx_v(st[1])
                elif st[0] == "scores":
                    scores(*st[1:])
                elif st[0] == "maxima":
                    maxima(*st[1:])
                elif st[0] == "probs":
                    probs_(*st[1:])
                elif st[0] == "pv":
                    pv(*st[1:])
                elif st[0] == "proj":
                    proj(*st[1:])
                elif st[0] == "up":
                    up(*st[1:])
                elif st[0] == "down":
                    down(*st[1:])

            for st in HEAD:
                stage(0, st)
            pe.wait_ge(w_loads, 16 * len(big))
            with pe.Fori(0, ITERS - 1) as it:
                for st, ahead in BODY:
                    stage(it + 1 if ahead else it, st)
            for st, ahead in BODY:
                if not ahead:
                    stage(ITERS - 1, st)


def constants():
    half = HD // 2
    inv = np.float32(1.0) / np.float32(10000.0) ** (np.arange(half, dtype=np.float32) / np.float32(half))
    ang = np.arange(N, dtype=np.float32)[None, :] * inv.astype(np.float32)[:, None]
    rows = np.array(CHANNELS[:P]) % HD
    sign = np.where(rows < half, -1.0, 1.0).astype(np.float32)[:, None]
    return {"ident": np.eye(P, dtype=np.float32), "cos": np.cos(ang)[rows % half].astype(np.float32), "sin": (np.sin(ang)[rows % half] * sign).astype(np.float32)}


def kernel(**inputs):
    from concourse import bacc
    from concourse.bass_utils import run_bass_kernel_spmd

    def a(name):
        return np.asarray(inputs[name])

    def in_order(w, *qk):
        order = np.arange(w.shape[-1])
        for at in qk:
            order[at:at + D] = at + np.array(CHANNELS)
        return np.ascontiguousarray(w[..., order])

    def by_tile(v, n):
        return np.ascontiguousarray(v.reshape(n, P).T)

    arrays = dict(constants())
    arrays["x"], arrays["ctx"] = a("x"), a("ctx_1024")
    arrays["ctxT"] = np.ascontiguousarray(a("ctx_1024").transpose(0, 2, 1))
    arrays["condT"] = np.ascontiguousarray(a("cond_1024").T)
    for new, old in (("w_mod0", "W_mod"), ("w_qkv0", "W_qkv"), ("w_proj0", "W_proj"), ("w_qc0", "W_qc"), ("w_kvc0", "W_kvc"),
                     ("w_cproj0", "W_cproj"), ("w_up0", "W_mlp1"), ("w_down0", "W_mlp2"), ("b_mod0", "b_mod"), ("b_qkv0", "b_qkv"),
                     ("b_proj0", "b_proj"), ("b_kvc0", "b_kvc"), ("b_cproj0", "b_cproj"), ("b_down0", "b_mlp2")):
        arrays[new] = a("L0_xcond_" + old)
    for new, old in (("w_qkv1", "qkv_w"), ("w_proj1", "sa_out_w"), ("w_qc1", "q_w"), ("w_cproj1", "ca_out_w"), ("w_up1", "ffn_w1"),
                     ("w_down1", "ffn_w2"), ("w_ln0", "ln1_w"), ("w_ln1", "ln2_w"), ("w_ln2", "ln3_w")):
        arrays[new] = np.ascontiguousarray(a("L1_xcond_" + old).T)
    arrays["w_kvc1"] = np.ascontiguousarray(np.concatenate([a("L1_xcond_k_w").T, a("L1_xcond_v_w").T], axis=1))
    for l in range(LAYERS):
        arrays[f"w_qkv{l}"] = in_order(arrays[f"w_qkv{l}"], 0, D)
        arrays[f"w_qc{l}"] = in_order(arrays[f"w_qc{l}"], 0)
        arrays[f"w_kvc{l}"] = in_order(arrays[f"w_kvc{l}"], 0)
    for i in range(SITES):
        arrays[f"b_ln{i}"] = a(f"L1_xcond_ln{i + 1}_b")
    arrays["b_down1"] = a("L1_xcond_ffn_b2")
    arrays["b_qk_cols"] = by_tile(in_order(a("L0_xcond_b_qkv"), 0, D)[0:2 * D], 2 * KT)
    arrays["b_qc_cols"] = by_tile(in_order(a("L0_xcond_b_qc"), 0), KT)
    arrays["b_kc_cols"] = by_tile(in_order(a("L0_xcond_b_kvc"), 0)[0:D], KT)
    arrays["b_up0_cols"] = by_tile(a("L0_xcond_b_mlp1"), FT)
    arrays["b_up1_cols"] = by_tile(a("L1_xcond_ffn_b1"), FT)

    nc = bacc.Bacc("TRN2", target_bir_lowering=False, num_devices=1)
    ins = {name: nc.dram_tensor("in_" + name, v.shape, mybir.dt.from_np(v.dtype), kind="ExternalInput").ap()
           for name, v in arrays.items()}
    out = nc.dram_tensor("out", (B, N, D), F32, kind="ExternalOutput").ap()
    build(nc, ins, out)
    r = run_bass_kernel_spmd(nc, [{"in_" + name: v for name, v in arrays.items()}], core_ids=[0])
    return r.results[0]["out"]
```
